# Optimizing a Trainium2 kernel written in Bass

```python
import numpy as np
import jax
import jax.numpy as jnp

def _softmax(x, axis=-1):
    return jax.nn.softmax(x, axis=axis)

def _gelu(x):
    return jax.nn.gelu(x, approximate=True)

def _silu(x):
    return jax.nn.silu(x)

def _sigmoid(x):
    return jax.nn.sigmoid(x)

def _layernorm(x, axis=-1, eps=1e-05):
    m = jnp.mean(x, axis=axis, keepdims=True)
    v = jnp.var(x, axis=axis, keepdims=True)
    return (x - m) / jnp.sqrt(v + eps)

def _scatter_add(tgt, idx, src, axis=0):
    return tgt.at[idx].add(src)

def _segment_sum(src, seg, n):
    return jax.ops.segment_sum(src, seg, n)
kernel_name = 'mk_hybrid_d1_jaxref_r8_ce396a'

def setup_inputs(seed: int=0):
    np.random.seed(seed)
    _w = jnp.asarray

    def _L0_attn_a_setup():
        import math
        import jax, jax.numpy as jnp
        import numpy as np
        H, KV, D = (16, 4, 128)
        HID = 256
        ROPE_BASE = 1000000.0
        EPS = 1e-06

        def _layernorm(x, w, b):
            mu = jnp.mean(x, axis=-1, keepdims=True)
            xc = x - mu
            var = jnp.mean(xc * xc, axis=-1, keepdims=True)
            return xc * jax.lax.rsqrt(var + EPS) * w + b

        def _rope(x, cos, sin):
            xr, xi = (x[..., 0::2], x[..., 1::2])
            c, s = (cos[None, None], sin[None, None])
            out = jnp.stack([xr * c - xi * s, xr * s + xi * c], axis=-1)
            return out.reshape(x.shape)
        key = jax.random.key(seed)
        ks = jax.random.split(key, 3)
        B, S = (2, 256)
        s = 0.02
        return {'x': jax.random.normal(ks[0], (B, S, HID), jnp.float32), 'w_qkv': jax.random.normal(ks[1], (2 * H * D + 2 * KV * D, HID), jnp.float32) * s, 'w_o': jax.random.normal(ks[2], (HID, H * D), jnp.float32) * s, 'q_norm_w': jnp.ones((D,), jnp.float32), 'q_norm_b': jnp.zeros((D,), jnp.float32), 'k_norm_w': jnp.ones((D,), jnp.float32), 'k_norm_b': jnp.zeros((D,), jnp.float32)}
    _L0_attn_a_in = _L0_attn_a_setup()

    def _L0_attn_b_setup():
        import jax, jax.numpy as jnp
        import numpy as np
        B, T, HID = (2, 256, 256)
        H, HKV = (16, 4)
        D = HID // H
        G = H // HKV
        ROPE_BASE = 1000000.0
        DTYPE = jnp.bfloat16

        def rotate_half(x):
            half = x.shape[-1] // 2
            return jnp.concatenate([-x[..., half:], x[..., :half]], axis=-1)
        key = jax.random.key(seed)
        ks = jax.random.split(key, 8)
        s = 0.02
        return {'x': jax.random.normal(ks[0], (B, T, HID), dtype=DTYPE), 'Wq': (jax.random.normal(ks[1], (HID, H * D), dtype=jnp.float32) * s).astype(DTYPE), 'bq': jnp.zeros((H * D,), dtype=DTYPE), 'Wk': (jax.random.normal(ks[2], (HID, HKV * D), dtype=jnp.float32) * s).astype(DTYPE), 'bk': jnp.zeros((HKV * D,), dtype=DTYPE), 'Wv': (jax.random.normal(ks[3], (HID, HKV * D), dtype=jnp.float32) * s).astype(DTYPE), 'bv': jnp.zeros((HKV * D,), dtype=DTYPE), 'Wo': (jax.random.normal(ks[4], (H * D, HID), dtype=jnp.float32) * s).astype(DTYPE)}
    _L0_attn_b_in = _L0_attn_b_setup()

    def _L0_ffn_setup():
        import jax, jax.numpy as jnp
        import numpy as np
        B, T, D = (1, 256, 256)
        E, K, F = (64, 4, 64)
        S, SF = (2, 64 * 4)
        CAP = 32

        def _moe_forward(x, router_w, router_bias, gate_w, up_w, down_w, sh_gate_w, sh_up_w, sh_down_w):
            b, t, d = x.shape
            flat = x.reshape(b * t, d)
            N = flat.shape[0]
            logits = flat @ router_w.T
            scores = jax.nn.softmax(logits, axis=-1)
            _, topk_idx = jax.lax.top_k(logits + router_bias, K)
            topk_w = jnp.take_along_axis(scores, topk_idx, axis=-1)
            topk_w = topk_w / topk_w.sum(axis=-1, keepdims=True)
            P = N * K
            e_flat = topk_idx.reshape(-1)
            t_flat = jnp.repeat(jnp.arange(N), K)
            w_flat = topk_w.reshape(-1)
            order = jnp.argsort(e_flat)
            e_s, t_s, w_s = (e_flat[order], t_flat[order], w_flat[order])
            counts = jnp.bincount(e_s, length=E)
            starts = jnp.concatenate([jnp.zeros((1,), counts.dtype), jnp.cumsum(counts)[:-1]])
            pos = jnp.arange(P) - starts[e_s]
            slot = jnp.where(pos < CAP, pos, CAP)
            tok_table = jnp.zeros((E, CAP + 1), jnp.int32).at[e_s, slot].set(t_s)[:, :CAP]
            w_table = jnp.zeros((E, CAP + 1), w_s.dtype).at[e_s, slot].set(w_s)[:, :CAP]
            xg = flat[tok_table]
            g = jnp.einsum('ecd,efd->ecf', xg, gate_w)
            u = jnp.einsum('ecd,efd->ecf', xg, up_w)
            y = jnp.einsum('ecf,edf->ecd', jax.nn.silu(g) * u, down_w)
            out = jnp.zeros_like(flat).at[tok_table.reshape(-1)].add((y * w_table[..., None]).reshape(-1, d))
            sg = jnp.einsum('nd,sfd->nsf', flat, sh_gate_w)
            su = jnp.einsum('nd,sfd->nsf', flat, sh_up_w)
            out = out + jnp.einsum('nsf,sdf->nd', jax.nn.silu(sg) * su, sh_down_w)
            return out.reshape(b, t, d)
        key = jax.random.key(seed)
        ks = jax.random.split(key, 9)
        s = 0.02
        return {'x': jax.random.normal(ks[0], (B, T, D), jnp.float32), 'router_w': jax.random.normal(ks[1], (E, D), jnp.float32) * s, 'router_bias': jnp.zeros((E,), jnp.float32), 'gate_w': jax.random.normal(ks[2], (E, F, D), jnp.float32) * s, 'up_w': jax.random.normal(ks[3], (E, F, D), jnp.float32) * s, 'down_w': jax.random.normal(ks[4], (E, D, F), jnp.float32) * s, 'sh_gate_w': jax.random.normal(ks[5], (S, SF, D), jnp.float32) * s, 'sh_up_w': jax.random.normal(ks[6], (S, SF, D), jnp.float32) * s, 'sh_down_w': jax.random.normal(ks[7], (S, D, SF), jnp.float32) * s}
    _L0_ffn_in = _L0_ffn_setup()
    _d = {'L0_attn_a_x': _L0_attn_a_in['x'], 'L0_attn_a_w_qkv': _L0_attn_a_in['w_qkv'], 'L0_attn_a_w_o': _L0_attn_a_in['w_o'], 'L0_attn_a_q_norm_w': _L0_attn_a_in['q_norm_w'], 'L0_attn_a_q_norm_b': _L0_attn_a_in['q_norm_b'], 'L0_attn_a_k_norm_w': _L0_attn_a_in['k_norm_w'], 'L0_attn_a_k_norm_b': _L0_attn_a_in['k_norm_b'], 'L0_attn_b_Wq': _L0_attn_b_in['Wq'], 'L0_attn_b_bq': _L0_attn_b_in['bq'], 'L0_attn_b_Wk': _L0_attn_b_in['Wk'], 'L0_attn_b_bk': _L0_attn_b_in['bk'], 'L0_attn_b_Wv': _L0_attn_b_in['Wv'], 'L0_attn_b_bv': _L0_attn_b_in['bv'], 'L0_attn_b_Wo': _L0_attn_b_in['Wo'], 'L0_ffn_router_w': _L0_ffn_in['router_w'], 'L0_ffn_router_bias': _L0_ffn_in['router_bias'], 'L0_ffn_gate_w': _L0_ffn_in['gate_w'], 'L0_ffn_up_w': _L0_ffn_in['up_w'], 'L0_ffn_down_w': _L0_ffn_in['down_w'], 'L0_ffn_sh_gate_w': _L0_ffn_in['sh_gate_w'], 'L0_ffn_sh_up_w': _L0_ffn_in['sh_up_w'], 'L0_ffn_sh_down_w': _L0_ffn_in['sh_down_w']}
    _x0 = _d['L0_attn_a_x']
    _d['L0_attn_a_x'] = jax.random.normal(jax.random.fold_in(jax.random.key(seed), 1), (2, 512, 256), dtype=_x0.dtype)
    del _x0
    return _d

def reference(L0_attn_a_x, L0_attn_a_w_qkv, L0_attn_a_w_o, L0_attn_a_q_norm_w, L0_attn_a_q_norm_b, L0_attn_a_k_norm_w, L0_attn_a_k_norm_b, L0_attn_b_Wq, L0_attn_b_bq, L0_attn_b_Wk, L0_attn_b_bk, L0_attn_b_Wv, L0_attn_b_bv, L0_attn_b_Wo, L0_ffn_router_w, L0_ffn_router_bias, L0_ffn_gate_w, L0_ffn_up_w, L0_ffn_down_w, L0_ffn_sh_gate_w, L0_ffn_sh_up_w, L0_ffn_sh_down_w):

    def _L0_attn_a_ref(x, w_qkv, w_o, q_norm_w, q_norm_b, k_norm_w, k_norm_b):
        import math
        import jax, jax.numpy as jnp
        import numpy as np
        H, KV, D = (16, 4, 128)
        HID = 256
        ROPE_BASE = 1000000.0
        EPS = 1e-06

        def _layernorm(x, w, b):
            mu = jnp.mean(x, axis=-1, keepdims=True)
            xc = x - mu
            var = jnp.mean(xc * xc, axis=-1, keepdims=True)
            return xc * jax.lax.rsqrt(var + EPS) * w + b

        def _rope(x, cos, sin):
            xr, xi = (x[..., 0::2], x[..., 1::2])
            c, s = (cos[None, None], sin[None, None])
            out = jnp.stack([xr * c - xi * s, xr * s + xi * c], axis=-1)
            return out.reshape(x.shape)
        B, S, _ = x.shape
        qkv = x @ w_qkv.T
        qg, k, v = jnp.split(qkv, [2 * H * D, 2 * H * D + KV * D], axis=-1)
        q, gate = jnp.split(qg, 2, axis=-1)
        q = q.reshape(B, S, H, D).transpose(0, 2, 1, 3)
        k = k.reshape(B, S, KV, D).transpose(0, 2, 1, 3)
        v = v.reshape(B, S, KV, D).transpose(0, 2, 1, 3)
        q = _layernorm(q, q_norm_w, q_norm_b)
        k = _layernorm(k, k_norm_w, k_norm_b)
        inv = 1.0 / ROPE_BASE ** (jnp.arange(0, D, 2, dtype=jnp.float32) / D)
        freqs = jnp.outer(jnp.arange(S, dtype=jnp.float32), inv)
        cos, sin = (jnp.cos(freqs), jnp.sin(freqs))
        q = _rope(q, cos, sin)
        k = _rope(k, cos, sin)
        rep = H // KV
        k = jnp.repeat(k, rep, axis=1)
        v = jnp.repeat(v, rep, axis=1)
        scores = jnp.einsum('bhqd,bhkd->bhqk', q, k) / math.sqrt(D)
        causal = jnp.tril(jnp.ones((S, S), bool))
        scores = jnp.where(causal[None, None], scores, -jnp.inf)
        attn = jax.nn.softmax(scores, axis=-1)
        out = jnp.einsum('bhqk,bhkd->bhqd', attn, v)
        out = out.transpose(0, 2, 1, 3).reshape(B, S, H * D)
        out = out * jax.nn.sigmoid(gate)
        return out @ w_o.T

    def _L0_attn_b_ref(x, Wq, bq, Wk, bk, Wv, bv, Wo):
        import jax, jax.numpy as jnp
        import numpy as np
        B, T, HID = (2, 256, 256)
        H, HKV = (16, 4)
        D = HID // H
        G = H // HKV
        ROPE_BASE = 1000000.0
        DTYPE = jnp.bfloat16

        def rotate_half(x):
            half = x.shape[-1] // 2
            return jnp.concatenate([-x[..., half:], x[..., :half]], axis=-1)
        b, t, _ = x.shape
        dt = x.dtype
        half = D // 2
        inv_freq = 1.0 / ROPE_BASE ** (jnp.arange(half, dtype=jnp.float32) / half)
        ang = jnp.outer(jnp.arange(t, dtype=jnp.float32), inv_freq)
        cos = jnp.concatenate([jnp.cos(ang), jnp.cos(ang)], axis=-1).astype(dt)[None, :, None, :]
        sin = jnp.concatenate([jnp.sin(ang), jnp.sin(ang)], axis=-1).astype(dt)[None, :, None, :]
        q = (x @ Wq + bq).reshape(b, t, H, D)
        k = (x @ Wk + bk).reshape(b, t, HKV, D)
        v = (x @ Wv + bv).reshape(b, t, HKV, D)
        q = q * cos + rotate_half(q) * sin
        k = k * cos + rotate_half(k) * sin
        qg = q.reshape(b, t, HKV, G, D)
        scale = D ** (-0.5)
        attn = jnp.einsum('bikgd,bjkd->bkgij', qg, k) * scale
        causal = jnp.tril(jnp.ones((t, t), dtype=bool))
        attn = jnp.where(causal, attn, jnp.finfo(dt).min)
        p = jax.nn.softmax(attn.astype(jnp.float32), axis=-1).astype(dt)
        out = jnp.einsum('bkgij,bjkd->bikgd', p, v).reshape(b, t, H * D)
        return out @ Wo

    def _L0_ffn_ref(x, router_w, router_bias, gate_w, up_w, down_w, sh_gate_w, sh_up_w, sh_down_w):
        import jax, jax.numpy as jnp
        import numpy as np
        B, T, D = (1, 256, 256)
        E, K, F = (64, 4, 64)
        S, SF = (2, 64 * 4)
        CAP = 32

        def _moe_forward(x, router_w, router_bias, gate_w, up_w, down_w, sh_gate_w, sh_up_w, sh_down_w):
            b, t, d = x.shape
            flat = x.reshape(b * t, d)
            N = flat.shape[0]
            logits = flat @ router_w.T
            scores = jax.nn.softmax(logits, axis=-1)
            _, topk_idx = jax.lax.top_k(logits + router_bias, K)
            topk_w = jnp.take_along_axis(scores, topk_idx, axis=-1)
            topk_w = topk_w / topk_w.sum(axis=-1, keepdims=True)
            P = N * K
            e_flat = topk_idx.reshape(-1)
            t_flat = jnp.repeat(jnp.arange(N), K)
            w_flat = topk_w.reshape(-1)
            order = jnp.argsort(e_flat)
            e_s, t_s, w_s = (e_flat[order], t_flat[order], w_flat[order])
            counts = jnp.bincount(e_s, length=E)
            starts = jnp.concatenate([jnp.zeros((1,), counts.dtype), jnp.cumsum(counts)[:-1]])
            pos = jnp.arange(P) - starts[e_s]
            slot = jnp.where(pos < CAP, pos, CAP)
            tok_table = jnp.zeros((E, CAP + 1), jnp.int32).at[e_s, slot].set(t_s)[:, :CAP]
            w_table = jnp.zeros((E, CAP + 1), w_s.dtype).at[e_s, slot].set(w_s)[:, :CAP]
            xg = flat[tok_table]
            g = jnp.einsum('ecd,efd->ecf', xg, gate_w)
            u = jnp.einsum('ecd,efd->ecf', xg, up_w)
            y = jnp.einsum('ecf,edf->ecd', jax.nn.silu(g) * u, down_w)
            out = jnp.zeros_like(flat).at[tok_table.reshape(-1)].add((y * w_table[..., None]).reshape(-1, d))
            sg = jnp.einsum('nd,sfd->nsf', flat, sh_gate_w)
            su = jnp.einsum('nd,sfd->nsf', flat, sh_up_w)
            out = out + jnp.einsum('nsf,sdf->nd', jax.nn.silu(sg) * su, sh_down_w)
            return out.reshape(b, t, d)
        return _moe_forward(x, router_w, router_bias, gate_w, up_w, down_w, sh_gate_w, sh_up_w, sh_down_w)
    x = L0_attn_a_x
    x = x + _L0_attn_a_ref(_layernorm(x, axis=-1), L0_attn_a_w_qkv, L0_attn_a_w_o, L0_attn_a_q_norm_w, L0_attn_a_q_norm_b, L0_attn_a_k_norm_w, L0_attn_a_k_norm_b)
    x = x + _L0_ffn_ref(_layernorm(x, axis=-1), L0_ffn_router_w, L0_ffn_router_bias, L0_ffn_gate_w, L0_ffn_up_w, L0_ffn_down_w, L0_ffn_sh_gate_w, L0_ffn_sh_up_w, L0_ffn_sh_down_w)
    x = x + _L0_attn_b_ref(_layernorm(x, axis=-1), L0_attn_b_Wq, L0_attn_b_bq, L0_attn_b_Wk, L0_attn_b_bk, L0_attn_b_Wv, L0_attn_b_bv, L0_attn_b_Wo)
    x = x + _L0_ffn_ref(_layernorm(x, axis=-1), L0_ffn_router_w, L0_ffn_router_bias, L0_ffn_gate_w, L0_ffn_up_w, L0_ffn_down_w, L0_ffn_sh_gate_w, L0_ffn_sh_up_w, L0_ffn_sh_down_w)
    return x

_drawn_inputs = setup_inputs


def setup_inputs(seed=0):
    import zlib

    import numpy as np

    out = dict(_drawn_inputs(seed))
    spreads = {'L0_attn_a_q_norm_w': (1.0, 0.6),
     'L0_attn_a_q_norm_b': (0.0, 0.8),
     'L0_attn_a_k_norm_w': (1.0, 0.6),
     'L0_attn_a_k_norm_b': (0.0, 0.8),
     'L0_attn_b_bq': (0.0, 0.8),
     'L0_attn_b_bk': (0.0, 0.8),
     'L0_attn_b_bv': (0.0, 0.1),
     'L0_ffn_router_bias': (0.0, 0.8)}
    factors = {'L0_attn_b_Wq': 8.0,
     'L0_attn_b_Wk': 8.0,
     'L0_attn_b_Wv': 4.438,
     'L0_ffn_router_w': 8.0,
     'L0_ffn_gate_w': 8.0,
     'L0_ffn_up_w': 8.0,
     'L0_ffn_down_w': 8.0}
    for name, (base, spread) in spreads.items():
        noise = np.random.default_rng([zlib.crc32(name.encode()), seed]).standard_normal(out[name].shape)
        drawn = base * np.exp(spread * noise) if base else spread * noise
        out[name] = jnp.asarray(drawn.astype(out[name].dtype))
    for name, factor in factors.items():
        out[name] = (out[name] * factor).astype(out[name].dtype)
    return out
```

```python
from contextlib import ExitStack

import numpy as np

import concourse.bass as bass
from concourse import mybir

F32 = mybir.dt.float32
BF16 = mybir.dt.bfloat16
U32 = mybir.dt.uint32
ACT = mybir.ActivationFunctionType
ALU = mybir.AluOpType
AX = mybir.AxisListType.X
ds = bass.ds

P = 128
B, S, D = 2, 512, 256
N = B * S
NT = N // P
ST = S // P
KT = D // P
LN_EPS, HEAD_EPS = 1e-5, 1e-6

H, KV, HD = 16, 4, 128
REP = H // KV
QC, KC = REP * HD, HD
COLS = QC + 2 * KC + QC

BH, BKV, BD = 16, 4, 16
BCOLS = (BH + 2 * BKV) * BD
SPLITS = 8

E, TOPK, F, CAP, SF = 64, 4, 64, 32, 512
SLOTS = E * CAP
EG = P // CAP
GROUPS = E // EG
LOW = 16300
ROUTE = 46
FT = SF // P
FAR = 4096.0

SCORE_AT = [2 * S - P, 2 * S, S, 0]
TURNED_AT = [0, S, 2 * S, 2 * S - P]
WIDE = 2 * S + 2 * P
IN_BANK = [[3], [2, 0], [1]]
NB = len(IN_BANK)


def program(nc, t, out):
    with ExitStack() as ctx:
        def sb(name, shape, dt=F32, stack=ctx):
            return stack.enter_context(nc.sbuf_tensor(name, shape, dt))

        def sem(name):
            return ctx.enter_context(nc.semaphore(name))

        ps = ctx.enter_context(nc.psum_tensor("ps", [P, 8, 512], F32))
        wide = ps[:, 4:7, :].rearrange("p a b -> p (a b)")

        x = sb("x_res", [P, NT, D])
        xn = sb("xn", [P, NT, D])
        xnT = sb("xnT", [P, KT, N])
        ident = sb("ident", [P, P])
        identb = sb("identb", [P, P], BF16)
        maskb = sb("maskb", [P, P], BF16)
        half = sb("half", [P, 8])
        ln_st = sb("ln_st", [P, NT, 6])
        ln_mv = sb("ln_mv", [P, NT, 2])
        ln_ve = sb("ln_ve", [P, NT])
        ln_rs = sb("ln_rs", [P, NT])
        sums = sb("sums", [P, 2, ST])
        negmax = sb("negmax", [P, 2, ST])
        rinv = sb("rinv", [P, ST])

        in_a = ExitStack()
        wo = sb("w_o", [P, H, D], F32, in_a)
        oT = sb("oT", [P, H, B, S], F32, in_a)
        wq = sb("w_qkvg", [P, 2, KT, COLS], F32, in_a)
        cosf = sb("cosf", [P, ST, HD], F32, in_a)
        sinf = sb("sinf", [P, ST, HD], F32, in_a)
        nvec = sb("nvec", [P, 4, HD], F32, in_a)
        rotA = sb("rotA", [P, 2, ST, HD], F32, in_a)
        rotB = sb("rotB", [P, 2, ST, HD], F32, in_a)
        biasT = sb("biasT", [P, 2, S], F32, in_a)
        nq = sb("nq", [P, REP + 1, HD], F32, in_a)
        ma = sb("ma", [P, REP + 1, HD], F32, in_a)
        mb = sb("mb", [P, REP + 1, HD], F32, in_a)
        hst = sb("hst", [P, REP + 1, 6], F32, in_a)
        hmv = sb("hmv", [P, REP + 1, 2], F32, in_a)
        hve = sb("hve", [P, REP + 1], F32, in_a)
        hneg = sb("hneg", [P, REP + 1], F32, in_a)
        hgo = sb("hgo", [P, 1], F32, in_a)
        hrs = sb("hrs", [P, REP + 1], F32, in_a)
        hnm = sb("hnm", [P, REP + 1], F32, in_a)
        qT = sb("qT", [P, 2, REP, S], F32, in_a)
        kT = sb("kT", [P, 2, S], F32, in_a)
        vA = sb("vA", [P, 2, ST, HD], F32, in_a)
        gate = sb("gate", [P, 2, ST, REP, HD], F32, in_a)
        pT = sb("pT", [P, WIDE], F32, in_a)
        probs = sb("probs", [P, WIDE], F32, in_a)
        oA = sb("oA", [P, ST, HD], F32, in_a)

        in_a.close()

        low = ExitStack()
        lg = sb("lg", [P, NT, E], F32, low)
        lb = sb("lb", [P, NT, E], F32, low)
        ex = sb("ex", [P, NT, E], F32, low)
        hot = sb("hot", [P, TOPK, NT, E], F32, low)
        prod = sb("prod", [P, TOPK, NT, E], F32, low)
        chosen = sb("chosen", [P, NT, E], BF16, low)
        top = sb("top", [P, NT, 8], F32, low)
        topi = sb("topi", [P, NT, 8], U32, low)
        rmax = sb("rmax", [P, NT], F32, low)
        rz = sb("rz", [P, 2, NT], F32, low)
        expert = sb("expert", [P, TOPK, NT], F32, low)
        place = sb("place", [P, TOPK, NT], F32, low)
        score = sb("score", [P, TOPK, NT], F32, low)
        share = sb("share", [P, TOPK, NT], F32, low)
        slot = sb("slot", [P, TOPK, NT], F32, low)
        kept = sb("kept", [P, TOPK, NT], F32, low)
        count = lb
        found_row = sb("found_row", [P, GROUPS], F32, low)
        token_of = sb("token_of", [P, GROUPS], U32, low)
        slot_of = sb("slot_of", [P, TOPK, NT], U32, low)
        hsh = sb("hsh", [P, FT, N], F32, low)
        xg = sb("xg", [P, GROUPS, D], F32, low)
        turn = sb("turn", [P, E * CAP // 2], F32, low)
        xgT = turn[:, 0:2 * D].rearrange("p (a k s) -> p a k s", a=2, k=KT)
        yg = turn[:, 2 * D:4 * D].rearrange("p (a d) -> p a d", a=2)
        mark = [v.bitcast(BF16).rearrange("p (e c) -> p e c", c=CAP) for v in (
            prod[:, 0:2].rearrange("p a n e -> p (a n e)"), prod[:, 2:4].rearrange("p a n e -> p (a n e)"),
            turn[:])]
        gact = sb("gact", [P, 2, F], F32, low)
        hg = sb("hg", [P, 2, 2, F], F32, low)
        hgT = sb("hgT", [P, 2, P], F32, low)
        gath = xg[:, 0:2 * TOPK].rearrange("p (a j) d -> p a j d", j=TOPK)
        hup = xg[:].rearrange("p g d -> p (g d)").rearrange("p (c s) -> p c s", s=S)
        low.close()

        low = ExitStack()
        bqs = sb("b_qs", [P, 2, BH, SPLITS, BD], BF16, low)
        bks = sb("b_ks", [P, 2, BKV, SPLITS, BD], BF16, low)
        bqT = sb("b_qT", [P, BH, S], BF16, low)
        bkT = sb("b_kT", [P, BKV, S], BF16, low)
        bv = sb("b_v", [P, ST, BKV, 32], F32, low)
        bvc = sb("b_vc", [P, ST, 32], F32, low)
        bp = sb("b_p", [P, 2, WIDE], F32, low)
        bpT = sb("b_pT", [P, 4, WIDE], F32, low)
        low.close()
        bflat = bpT[:].rearrange("p a b -> p (a b)")
        QW, KW = BH * BD, BKV * BD
        PAIR = 2 * (QW + KW)
        bt1, bt2, brot, br1 = [bflat[:, i * PAIR:(i + 1) * PAIR] for i in range(4)]
        bp1, bp2, bp3 = [bflat[:, 4 * PAIR + i * PAIR // 2:4 * PAIR + (i + 1) * PAIR // 2].bitcast(BF16) for i in range(3)]
        bqkv = bflat[:, 11 * PAIR // 2:11 * PAIR // 2 + ST * BCOLS].rearrange("p (n c) -> p n c", c=BCOLS)
        boT = xn[:].rearrange("p n d -> p (n d)").rearrange("p (k s) -> p k s", s=S)
        sb("low_area", [P, LOW])
        wd = sb("w_down", [P, E // 2, D])
        wsg = sb("w_sgate", [P, KT, SF])
        wsu = sb("w_sup", [P, KT, SF])
        wsd = sb("w_sdown", [P, FT, D])
        wr = sb("w_router", [P, KT, E])
        rbias = sb("rbias", [P, E])
        iota = sb("iota", [P, E])
        near = sb("near", [P, CAP])
        nought = sb("nought", [P, 2 * GROUPS], BF16)
        number = sb("number", [P, NT, 2], BF16)
        parity = sb("parity", [P, 2])
        tri = sb("tri", [P, P], BF16)
        ones = sb("ones", [P, P], BF16)
        wgu = sb("w_gateup", [P, KT, E, 2 * F])

        wb = sb("w_bqkv", [P, KT, BCOLS])
        wob = sb("w_bo", [P, BKV, D])
        bb = sb("b_bias", [P, BCOLS], BF16)
        bcos = sb("b_cos", [P, ST, 2, BD])
        bsin = sb("b_sin", [P, ST, 2, BD])

        xn_dram = nc.dram_tensor("xn_rows", [N, D], F32).ap()
        y_dram = nc.dram_tensor("y_rows", [SLOTS, D], F32).ap()

        ld_x = [sem(f"ld_x{i}") for i in range(2)]
        ld_const = sem("ld_const")
        ld_wq = [sem(f"ld_wq{i}") for i in range(2)]
        ld_wo = sem("ld_wo")
        half_ready = sem("half_ready")
        ln_stats = sem("ln_stats")
        ln_aggr = sem("ln_aggr")
        ln_var = sem("ln_var")
        ln_rstd = sem("ln_rstd")
        xn_ready = sem("xn_ready")
        xn_turned = sem("xn_turned")
        xnT_ready = sem("xnT_ready")
        tab_step = sem("tab_step")
        tab_turned = sem("tab_turned")
        tab_ready = sem("tab_ready")
        q_mm = sem("q_mm")
        kv_mm = sem("kv_mm")
        gate_mm = sem("gate_mm")
        gate_done = sem("gate_done")
        gate_half = sem("gate_half")
        v_done = sem("v_done")
        st_step = sem("st_step")
        st_done = sem("st_done")
        head_pow = sem("head_pow")
        head_rs = sem("head_rs")
        norm_done = sem("norm_done")
        rotA_done = sem("rotA_done")
        rotB_done = sem("rotB_done")
        rope_done = sem("rope_done")
        qk_turned = sem("qk_turned")
        qkT_done = sem("qkT_done")
        s_mm = sem("s_mm")
        max_done = sem("max_done")
        exp_done = sem("exp_done")
        p_turned = sem("p_turned")
        pT_done = sem("pT_done")
        pv_mm = sem("pv_mm")
        rinv_done = sem("rinv_done")
        o_done = sem("o_done")
        o_turned = sem("o_turned")
        oT_done = sem("oT_done")
        wo_mm = sem("wo_mm")
        x_added = sem("x_added")
        stored = sem("stored")
        ld_sh = sem("ld_sh")
        ld_gu = sem("ld_gu")
        ld_dn = sem("ld_dn")
        xn_out = sem("xn_out")
        counted = sem("counted")
        marked = sem("marked")
        row_found = sem("row_found")
        mark_used = sem("mark_used")
        tokens_ready = sem("tokens_ready")
        r_mm = sem("r_mm")
        route = sem("route")
        shifted = sem("shifted")
        ex_done = sem("ex_done")
        chosen_done = sem("chosen_done")
        pos_mm = sem("pos_mm")
        slots_ready = sem("slots_ready")
        sh_mm = sem("sh_mm")
        sh_act = sem("sh_act")
        sh_up = sem("sh_up")
        sh_h = sem("sh_h")
        sd_mm = sem("sd_mm")
        sd_add = sem("sd_add")
        xg_in = [sem(f"xg_in{g}") for g in range(GROUPS)]
        xg_turned = sem("xg_turned")
        xgT_done = sem("xgT_done")
        gu_mm = sem("gu_mm")
        gact_done = sem("gact_done")
        hg_done = sem("hg_done")
        hg_turned = sem("hg_turned")
        hgT_done = sem("hgT_done")
        dn_mm = sem("dn_mm")
        yg_done = sem("yg_done")
        y_out = [sem(f"y_out{i}") for i in range(2)]
        rows_in = [sem(f"rows_in{i}") for i in range(2)]
        mixed = sem("mixed")
        ld_b = sem("ld_b")
        ld_bw = sem("ld_bw")
        bv_zero = sem("bv_zero")
        b_mm = sem("b_mm")
        b_qkv = sem("b_qkv")
        b_cosp = sem("b_cosp")
        b_sinp = sem("b_sinp")
        b_rot = sem("b_rot")
        b_step = sem("b_step")
        b_parts = sem("b_parts")
        b_v = sem("b_v")
        b_stack = sem("b_stack")
        b_turned = sem("b_turned")
        b_qkT = sem("b_qkT")
        b_s = sem("b_s")
        b_max = sem("b_max")
        b_exp = sem("b_exp")
        b_rinv = sem("b_rinv")
        b_norm = sem("b_norm")
        b_vc = sem("b_vc")
        b_pturned = sem("b_pturned")
        b_pT = sem("b_pT")
        b_pv = sem("b_pv")
        b_oT = sem("b_oT")
        b_wo = sem("b_wo")

        TILES, HEADS = 2 * KV * ST, 2 * KV * REP
        LAST = HEADS + REP + 1

        def steps(eng, body):
            first = REP + 2
            for s in range(first):
                body(s, s)
            with eng.Fori(0, KV - 1) as i:
                for c in range(8):
                    body(i * 8 + (first + c), first + c, i)
            for s in range(first + 8 * (KV - 1), LAST):
                body(s, s)

        def small_steps(eng, b, body):
            for u in range(6):
                body(b * BH + u, u)
            with eng.Fori(0, BKV - 2) as i:
                for c in range(4):
                    body(i * 4 + (b * BH + 6 + c), 6 + c, i)
            for u in range(BH - 2, BH + 2):
                body(b * BH + u, u)

        TURN_BANKS = ((2, 3, 7), (6, 0, 1))

        MARKED_BY = (0, 0, 0, 1, 2, 4, 6, 8)

        def bank_set(u):
            first = 4 * (u % 2)
            return ps[:, first:first + NB, :].rearrange("p a b -> p (a b)")

        def key_head(r, i):
            return r // 4 if i is None else i + r // 4

        def group_of(r, i):
            return r // 8 if i is None else i + r // 8

        block = ctx.enter_context(nc.Block())

        @block.sync
        def _(sp):
            sp.dma_start(x[:, 0:ST, :], t["x"][0].rearrange("(n p) d -> p n d", p=P)).then_inc(ld_x[0], 16)
            sp.dma_start(x[:, ST:NT, :], t["x"][1].rearrange("(n p) d -> p n d", p=P)).then_inc(ld_x[1], 16)
            sp.dma_start(ident[:], t["ident"]).then_inc(ld_const, 16)
            sp.dma_start(cosf[:], t["cosf"]).then_inc(ld_const, 16)
            sp.dma_start(sinf[:], t["sinf"]).then_inc(ld_const, 16)
            sp.dma_start(nvec[:], t["nvec"]).then_inc(ld_const, 16)
            sp.dma_start(identb[:], t["identb"]).then_inc(ld_const, 16)
            sp.dma_start(maskb[:], t["maskb"]).then_inc(ld_const, 16)
            for g in range(KV):
                if g >= 2:
                    sp.wait_ge(gate_mm, 8 * (g - 1))
                sp.dma_start(wq[:, g % 2], t["w_qkvg"][g]).then_inc(ld_wq[g % 2], 16)
                if g == 1:
                    sp.dma_start(wo[:], t["w_o"]).then_inc(ld_wo, 16)
            sp.wait_ge(oT_done, HEADS)
            for tile, name in ((wsg, "w_sgate"), (wsu, "w_sup"), (wsd, "w_sdown"), (wr, "w_router"),
                               (rbias, "rbias"), (iota, "iota"), (near, "near"), (number, "number"), (nought, "nought"), (parity, "parity"), (tri, "tri"), (ones, "ones")):
                sp.dma_start(tile[:], t[name]).then_inc(ld_sh, 16)
            sp.dma_start(wgu[:], t["w_gateup"]).then_inc(ld_gu, 16)
            sp.wait_ge(wo_mm, NT)
            sp.dma_start(wd[:], t["w_down"]).then_inc(ld_dn, 16)

            for tile, name in ((bb, "b_bias"), (bcos, "b_cos"), (bsin, "b_sin")):
                sp.dma_start(tile[:], t[name]).then_inc(ld_b, 16)

            def experts(l):
                sp.wait_ge(xn_ready, (2 * l + 2) * NT)
                if l > 0:
                    for g in range(GROUPS):
                        sp.wait_ge(xg_in[g], l * 16)
                sp.dma_start(xn_dram.rearrange("(n p) d -> p n d", p=P), xn[:]).then_inc(xn_out, 16)
                for g in range(GROUPS):
                    sp.wait_ge(yg_done, l * GROUPS + g + 1)
                    sp.dma_start(y_dram[g * P:(g + 1) * P, :], yg[:, g % 2]).then_inc(y_out[g % 2], 16)

            experts(0)
            experts(1)
            sp.wait_ge(x_added, NT * 4)
            sp.dma_start(out.rearrange("b (n p) d -> p (b n) d", p=P), x[:]).then_inc(stored, 16)
            sp.wait_ge(stored, 16)

        @block.gpsimd
        def _(pool):
            pool.memset(half[:], -0.5).then_inc(half_ready, 1)
            pool.wait_ge(half_ready, 1)

            def layernorm(r):
                pool.wait_ge(ln_var, r + 1)
                pool.tensor_tensor(ln_rs[:], ln_ve[:], half[:, 0:NT], ALU.pow).then_inc(ln_rstd, 1)

            layernorm(0)

            def step(s, r, i=None):
                if r < TILES:
                    pool.wait_ge(st_done, 2 * (s + 1))
                    pool.tensor_tensor(hrs[:], hve[:], half[:, 0:REP + 1], ALU.pow).then_inc(head_pow, 1)
                    pool.wait_ge(head_pow, s + 1)
                    pool.tensor_tensor(hnm[:], hneg[:], hrs[:], ALU.mult).then_inc(head_rs, 1)
                    n = r % ST
                    pool.wait_ge(norm_done, (s + 1) * (REP + 1))
                    if r >= 1:
                        pool.wait_ge(rope_done, s)
                    pool.tensor_tensor(ma[:, 0:REP], nq[:, 0:REP], rotA[:, 0, n:n + 1].broadcast_to([P, REP, HD]),
                                       ALU.mult).then_inc(rotA_done, 1)
                    pool.tensor_tensor(ma[:, REP], nq[:, REP], rotA[:, 1, n], ALU.mult).then_inc(rotA_done, 1)

            pool.wait_ge(tab_ready, 1)
            steps(pool, step)

            def small_heads():
                layernorm(2)
                pool.memset(bv[:], 0.0).then_inc(bv_zero, 1)
                pool.wait_ge(ld_b, 3 * 16)
                for q in range(NT // 2):
                    pool.wait_ge(b_qkv, q + 1)
                    if q > 0:
                        pool.wait_ge(b_rot, q)
                    for n in range(2):
                        for c, (at, w) in enumerate(((0, QW), (QW, KW))):
                            heads = lambda v: v.rearrange("p (h d) -> p h d", d=BD)
                            tile = (q % 2) * 2 + n
                            pool.tensor_tensor(heads(bt1[:, 2 * at + n * w:2 * at + (n + 1) * w]), heads(bqkv[:, tile, at:at + w]),
                                               bcos[:, tile, c:c + 1].broadcast_to([P, w // BD, BD]), ALU.mult).then_inc(b_cosp, 1)

            def experts(l):
                def hidden(c):
                    pool.wait_ge(sh_act, l * 8 + c + 1)
                    pool.wait_ge(sh_up, l * 8 + c + 1)
                    at = hsh[:, c % FT, (c // FT) * S:(c // FT + 1) * S]
                    pool.tensor_tensor(at, at, hup[:, c], ALU.mult).then_inc(sh_h, 1)

                if l == 0:
                    pool.wait_ge(wo_mm, NT)
                    pool.dma_start(wb[:], t["w_bqkv"]).then_inc(ld_bw, 16)
                    pool.dma_start(wob[:], t["w_bo"]).then_inc(ld_bw, 16)
                layernorm(2 * l + 1)
                for c in range(8):
                    hidden(c)
                pool.wait_ge(tokens_ready, l + 1)
                pool.wait_ge(xn_out, (l + 1) * 16)
                pool.wait_ge(sh_h, (l + 1) * 8)
                for g in range(GROUPS):
                    pool.indirect_dma_start(
                        out=xg[:, g], out_offset=None, in_=xn_dram,
                        in_offset=bass.IndirectOffsetOnAxis(ap=token_of[:, g:g + 1], axis=0),
                        bounds_check=N - 1, oob_is_err=False).then_inc(xg_in[g], 16)
                for i in range(2):
                    pool.wait_ge(y_out[i], (l + 1) * GROUPS // 2 * 16)
                pool.wait_ge(slots_ready, l + 1)
                for n in range(NT):
                    if n >= 2 or l > 0:
                        pool.wait_ge(x_added, 2 * l * NT + NT + n - 1)
                    for j in range(TOPK):
                        pool.indirect_dma_start(
                            out=gath[:, n % 2, j], out_offset=None, in_=y_dram,
                            in_offset=bass.IndirectOffsetOnAxis(ap=slot_of[:, j, n:n + 1], axis=0),
                            bounds_check=SLOTS - 1, oob_is_err=False).then_inc(rows_in[n % 2], 16)

            experts(0)
            small_heads()
            experts(1)

        @block.scalar
        def _(act):
            def xnT_copies(r):
                for c in range(NT // 2):
                    act.wait_ge(xn_turned, r * NT + 2 * c + 2)
                    nc.scalar.copy(xnT[:, :, c * 2 * P:(c + 1) * 2 * P].rearrange("p k (n q) -> p n k q", n=2),
                                   ps[:, c, :].rearrange("p (n k q) -> p n k q", n=2, k=KT)).then_inc(xnT_ready, 1)

            xnT_copies(0)
            for c in range(2):
                act.wait_ge(tab_turned, c + 1)
                nc.scalar.copy(biasT[:, c], ps[:, 4 + c, :]).then_inc(tab_ready, 1)

            def step(s, r, i=None):
                if r < TILES:
                    st, n = (r // ST) % 2, r % ST
                    act.wait_ge(head_rs, s + 1)
                    if r >= 1:
                        act.wait_ge(rope_done, s)
                    for h in range(REP + 1):
                        src = ps[:, 0, h * HD:(h + 1) * HD] if h < REP else ps[:, 1, 0:HD]
                        nc.scalar.activation(nq[:, h], src, ACT.Identity, bias=hnm[:, h:h + 1],
                                             scale=hrs[:, h:h + 1]).then_inc(norm_done, 1)
                if r >= REP and r < LAST - 1:
                    k = s - REP
                    kp = r % 2
                    if r >= REP + 1:
                        act.wait_ge(p_turned, k)
                    for bank, tiles in enumerate(IN_BANK):
                        act.wait_ge(max_done, k * NB + bank + 1)
                        for i4 in tiles:
                            at = SCORE_AT[i4]
                            op = nc.scalar.activation(probs[:, at:at + (i4 + 1) * P], wide[:, at:at + (i4 + 1) * P],
                                                      ACT.Exp, bias=negmax[:, kp, i4:i4 + 1],
                                                      accum_out=sums[:, kp, i4:i4 + 1])
                        op.then_inc(exp_done, 1)
                if r < TILES:
                    act.wait_ge(kv_mm, s + 1)
                    if r >= REP + 1:
                        act.wait_ge(pv_mm, s - REP)
                    nc.scalar.copy(vA[:, st, n], ps[:, 1, KC:2 * KC]).then_inc(v_done, 1)
                    act.wait_ge(gate_mm, s + 1)
                    if r >= REP + 1:
                        act.wait_ge(o_done, (s - REP) * ST)
                    nc.scalar.activation(gate[:, st, n].rearrange("p h d -> p (h d)"), ps[:, 2, :], ACT.Tanh,
                                         scale=0.5).then_inc(gate_done, 1)
                if r >= REP and r < LAST - 1:
                    act.wait_ge(p_turned, s - REP + 1)
                    for a, b in ((0, S), (S, 2 * S), (2 * S, WIDE)):
                        nc.scalar.copy(pT[:, a:b], wide[:, a:b]).then_inc(pT_done, 1)
                if r >= REP + 1:
                    k5 = r - REP - 1
                    act.wait_ge(o_turned, s - REP)
                    g = group_of(k5, i)
                    dst = oT[:, ds(g * REP + k5 % REP, 1), (k5 // REP) % 2, :] if i is not None else \
                        oT[:, g * REP + k5 % REP:g * REP + k5 % REP + 1, (k5 // REP) % 2, :]
                    nc.scalar.copy(dst.rearrange("p a b -> p (a b)"), ps[:, 7, :]).then_inc(oT_done, 1)

            steps(act, step)

            def small_heads():
                xnT_copies(2)
                act.wait_ge(bv_zero, 1)

                def step(s, r, i=None):
                    if r < BH:
                        if r >= 2:
                            act.wait_ge(b_pturned, s - 1)
                        kp = r % 2
                        banks = bank_set(r)
                        for bank, tiles in enumerate(IN_BANK):
                            act.wait_ge(b_max, s * NB + bank + 1)
                            for i4 in tiles:
                                at = SCORE_AT[i4]
                                op = nc.scalar.activation(bp[:, kp, at:at + (i4 + 1) * P], banks[:, at:at + (i4 + 1) * P],
                                                          ACT.Exp, bias=negmax[:, kp, i4:i4 + 1],
                                                          accum_out=sums[:, kp, i4:i4 + 1])
                            op.then_inc(b_exp, 1)
                    if 1 <= r <= BH:
                        act.wait_ge(b_pturned, s)
                        banks = bank_set(r - 1)
                        for a, z in ((0, S), (S, 2 * S), (2 * S, WIDE)):
                            nc.scalar.copy(bpT[:, (r - 1) % 4, a:z], banks[:, a:z]).then_inc(b_pT, 1)
                    if r >= 5 and (r - 2) % 4 == 3:
                        g = key_head(r - 5, i)
                        act.wait_ge(b_pv, g + (b * BKV + 1))
                        dst = boT[:, g] if i is None else boT[:, ds(g, 1)].rearrange("p a b -> p (a b)")
                        nc.scalar.copy(dst, ps[:, 3, :]).then_inc(b_oT, 1)

                for b in range(B):
                    for q in range(2 * b, 2 * b + 2):
                        act.wait_ge(b_qkv, q + 1)
                        n = (q % 2) * 2
                        nc.scalar.copy(bv[:, n:n + 2, :, 0:BD], bqkv[:, n:n + 2, QW + KW:]
                                       .rearrange("p n (h d) -> p n h d", d=BD)).then_inc(b_v, 1)
                    for n in range(ST):
                        act.wait_ge(b_turned, b * ST + n + 1)
                        banks = TURN_BANKS[n % 2]
                        for c in range(2):
                            nc.scalar.copy(bqT[:, 8 * c:8 * c + 8, n * P:(n + 1) * P],
                                           ps[:, banks[c], :].bitcast(BF16).rearrange("p (h q) -> p h q", q=P)).then_inc(b_qkT, 1)
                        nc.scalar.copy(bkT[:, :, n * P:(n + 1) * P],
                                       ps[:, banks[2], 0:2 * P].bitcast(BF16).rearrange("p (h q) -> p h q", q=P)).then_inc(b_qkT, 1)
                    small_steps(act, b, step)

            def experts(l):
                xnT_copies(2 * l + 1)
                act.wait_ge(shifted, l + 1)
                nc.scalar.activation(ex[:], lg[:], ACT.Exp).then_inc(ex_done, 1)
                for c in range(8):
                    act.wait_ge(sh_mm, (l * 8 + c + 1) * 2 - 1)
                    nc.scalar.activation(hsh[:, c % FT, (c // FT) * S:(c // FT + 1) * S], ps[:, c % 2, :],
                                         ACT.Silu).then_inc(sh_act, 1)
                    act.wait_ge(sh_mm, (l * 8 + c + 1) * 2)
                    if l > 0 and c == 0:
                        act.wait_ge(x_added, (2 * l + 1) * NT)
                    nc.scalar.copy(hup[:, c], ps[:, 2 + c % 2, :]).then_inc(sh_up, 1)
                for it in range(GROUPS + 2):
                    if it < GROUPS:
                        g, u = it, l * GROUPS + it
                        act.wait_ge(xg_turned, u + 1)
                        nc.scalar.copy(xgT[:, g % 2].rearrange("p k s -> p (k s)"),
                                       ps[:, g % 2, 0:KT * P]).then_inc(xgT_done, 1)
                    if 1 <= it <= GROUPS:
                        g, u = it - 1, l * GROUPS + it - 1
                        act.wait_ge(gu_mm, u + 1)
                        if g >= 2:
                            act.wait_ge(hg_done, 2 * u - 2)
                        nc.scalar.activation(gact[:, g % 2], ps[:, 2 + g % 2, 0:F], ACT.Silu).then_inc(gact_done, 1)
                    if it >= 2:
                        g, u = it - 2, l * GROUPS + it - 2
                        act.wait_ge(hg_turned, u + 1)
                        nc.scalar.copy(hgT[:, g % 2], ps[:, 4, 0:P]).then_inc(hgT_done, 1)

            experts(0)
            small_heads()
            experts(1)

        @block.vector
        def _(dve):
            def layernorm(r):
                for n in range(NT):
                    if r == 0 and n % ST == 0:
                        dve.wait_ge(ld_x[n // ST], 16)
                    if r > 0:
                        dve.wait_ge(x_added, (r - 1) * NT + n + 1)
                    dve.bn_stats(ln_st[:, n], x[:, n]).then_inc(ln_stats, 1)
                for n in range(NT):
                    dve.wait_ge(ln_stats, r * NT + n + 1)
                    dve.bn_aggr(ln_mv[:, n], ln_st[:, n]).then_inc(ln_aggr, 1)
                dve.wait_ge(ln_aggr, (r + 1) * NT)
                dve.tensor_scalar(ln_ve[:], ln_mv[:, :, 1], LN_EPS, None, ALU.add).then_inc(ln_var, 1)
                dve.wait_ge(ln_rstd, r + 1)
                for n in range(NT):
                    dve.tensor_scalar(xn[:, n], x[:, n], ln_mv[:, n, 0:1], ln_rs[:, n:n + 1], ALU.subtract,
                                      ALU.mult).then_inc(xn_ready, 1)

            layernorm(0)

            dve.wait_ge(ld_const, 6 * 16)
            dve.tensor_scalar(nvec[:, 0:2], nvec[:, 0:2], HD ** -0.5, None, ALU.mult).then_inc(tab_step, 1)
            dve.wait_ge(tab_step, 1)

            def over_tiles(v, swapped=False):
                v = v.rearrange("p (a b) -> p a b", a=2)
                v = v[:, ::-1, :] if swapped else v
                return v.unsqueeze(1).broadcast_to([P, ST, 2, HD // 2])

            halves = lambda a: a.rearrange("p n (a b) -> p n a b", a=2)
            done = 1
            for c in range(2):
                w, b = nvec[:, 2 * c], nvec[:, 2 * c + 1]
                dve.tensor_tensor(halves(rotA[:, c]), halves(cosf[:]), over_tiles(w), ALU.mult).then_inc(tab_step, 1)
                dve.tensor_tensor(halves(rotB[:, c]), halves(sinf[:]), over_tiles(w, True), ALU.mult).then_inc(tab_step, 1)
                if c == 1:
                    dve.wait_ge(tab_turned, 1)
                ta, tb = gate[:, 0, 0], gate[:, 0, 1]
                dve.tensor_tensor(halves(ta), halves(cosf[:]), over_tiles(b), ALU.mult).then_inc(tab_step, 1)
                dve.tensor_tensor(halves(tb), halves(sinf[:]), over_tiles(b, True), ALU.mult).then_inc(tab_step, 1)
                done += 4
                dve.wait_ge(tab_step, done)
                dve.tensor_tensor(ta, ta, tb, ALU.add).then_inc(tab_step, 1)
                done += 1

            def step(s, r, i=None):
                if 1 <= r <= TILES:
                    m = r - 1
                    st, n = (m // ST) % 2, m % ST
                    if r == 1:
                        dve.wait_ge(tab_ready, 2)
                    dve.wait_ge(qk_turned, s)
                    dve.tensor_tensor(qT[:, st, :, n * P:(n + 1) * P], ps[:, 3, :].rearrange("p (h q) -> p h q", h=REP),
                                      biasT[:, 0:1, n * P:(n + 1) * P].broadcast_to([P, REP, P]), ALU.add).then_inc(qkT_done, 1)
                    dve.tensor_tensor(kT[:, st, n * P:(n + 1) * P], ps[:, 2, 0:P], biasT[:, 1, n * P:(n + 1) * P],
                                      ALU.add).then_inc(qkT_done, 1)
                    dve.wait_ge(gate_done, s)
                    g = gate[:, st, n].rearrange("p h d -> p (h d)")
                    dve.tensor_scalar(g, g, 0.5, 0.5, ALU.mult, ALU.add).then_inc(gate_half, 1)
                if r < TILES:
                    n = r % ST
                    J = REP + 1
                    dve.wait_ge(q_mm, s + 1)
                    for h in range(J):
                        if h == REP:
                            dve.wait_ge(kv_mm, s + 1)
                        src = ps[:, 0, h * HD:(h + 1) * HD] if h < REP else ps[:, 1, 0:HD]
                        dve.bn_stats(hst[:, h], src).then_inc(st_step, 1)
                    dve.wait_ge(st_step, s * 2 * J + J)
                    dve.tensor_copy(hgo[:], hst[:, 0, 0:1])
                    for h in range(J):
                        dve.bn_aggr(hmv[:, h], hst[:, h]).then_inc(st_step, 1)
                    dve.wait_ge(st_step, (s + 1) * 2 * J)
                    dve.tensor_scalar(hve[:], hmv[:, :, 1], HEAD_EPS, None, ALU.add).then_inc(st_done, 1)
                    dve.tensor_scalar(hneg[:], hmv[:, :, 0], -1.0, None, ALU.mult).then_inc(st_done, 1)
                if r >= REP and r < LAST - 1:
                    k = s - REP
                    for bank, tiles in enumerate(IN_BANK):
                        dve.wait_ge(s_mm, k * NB + bank + 1)
                        for i4 in tiles:
                            at = SCORE_AT[i4]
                            op = dve.tensor_reduce(negmax[:, r % 2, i4:i4 + 1], wide[:, at:at + (i4 + 1) * P], AX,
                                                   ALU.max, negate=True)
                        op.then_inc(max_done, 1)
                if r < TILES:
                    dve.wait_ge(norm_done, (s + 1) * J)
                    swapped = lambda a: a.rearrange("p h (a b) -> p h a b", a=2)[:, :, ::-1, :]
                    plain = lambda a: a.rearrange("p h (a b) -> p h a b", a=2)
                    dve.tensor_tensor(plain(mb[:, 0:REP]), swapped(nq[:, 0:REP]),
                                      plain(rotB[:, 0, n:n + 1]).broadcast_to([P, REP, 2, HD // 2]), ALU.mult).then_inc(rotB_done, 1)
                    dve.tensor_tensor(plain(mb[:, REP:J]), swapped(nq[:, REP:J]), plain(rotB[:, 1, n:n + 1]),
                                      ALU.mult).then_inc(rotB_done, 1)
                if r >= REP + 1:
                    k5 = r - REP - 1
                    st, h, kp = (k5 // REP) % 2, k5 % REP, k5 % 2
                    dve.wait_ge(exp_done, (s - REP) * NB)
                    if r >= REP + 2:
                        dve.wait_ge(o_done, (s - REP - 1) * ST)
                    dve.reciprocal(rinv[:], sums[:, kp]).then_inc(rinv_done, 1)
                    dve.wait_ge(pv_mm, s - REP)
                    dve.wait_ge(rinv_done, s - REP)
                    if r >= REP + 2:
                        dve.wait_ge(o_turned, s - REP - 1)
                    for i4 in range(ST):
                        dve.scalar_tensor_tensor(out=oA[:, i4], in0=ps[:, 7, i4 * HD:(i4 + 1) * HD],
                                                 scalar=rinv[:, i4:i4 + 1], in1=gate[:, st, i4, h], op0=ALU.mult,
                                                 op1=ALU.mult).then_inc(o_done, 1)
                if r < TILES:
                    dve.wait_ge(rotA_done, (s + 1) * 2)
                    dve.wait_ge(rotB_done, (s + 1) * 2)
                    dve.tensor_tensor(mb[:], ma[:], mb[:], ALU.add).then_inc(rope_done, 1)

            steps(dve, step)

            for n in range(NT):
                dve.wait_ge(wo_mm, n + 1)
                dve.tensor_tensor(x[:, n], x[:, n], ps[:, n % 4, 0:D], ALU.add).then_inc(x_added, 1)

            def small_heads():
                layernorm(2)
                dve.wait_ge(ld_b, 3 * 16)

                def step(s, r, i=None):
                    if r < BH:
                        banks = bank_set(r)
                        for bank, tiles in enumerate(IN_BANK):
                            dve.wait_ge(b_s, s * NB + bank + 1)
                            for i4 in tiles:
                                at = SCORE_AT[i4]
                                op = dve.tensor_reduce(negmax[:, r % 2, i4:i4 + 1], banks[:, at:at + (i4 + 1) * P], AX,
                                                       ALU.max, negate=True)
                            op.then_inc(b_max, 1)
                    if r < BH:
                        kp = r % 2
                        dve.wait_ge(b_exp, (s + 1) * NB)
                        if r >= 1 or b > 0:
                            dve.wait_ge(b_norm, s * ST)
                        dve.reciprocal(rinv[:], sums[:, kp]).then_inc(b_rinv, 1)
                        dve.wait_ge(b_rinv, s + 1)
                        for i4 in range(ST):
                            at = SCORE_AT[i4]
                            dve.tensor_scalar(bp[:, kp, at:at + (i4 + 1) * P], bp[:, kp, at:at + (i4 + 1) * P],
                                              rinv[:, i4:i4 + 1], None, ALU.mult).then_inc(b_norm, 1)
                    if r % 4 == 3:
                        g = key_head(r, i)
                        dve.wait_ge(b_v, 2 * b + 2)
                        if r > 3 or b > 0:
                            dve.wait_ge(b_pv, g + b * BKV)
                        src = bv[:, :, g] if i is None else bv[:, :, ds(g, 1)].rearrange("p a b c -> p a (b c)")
                        dve.tensor_copy(bvc[:], src).then_inc(b_vc, 1)

                for b in range(B):
                    for q in range(2 * b, 2 * b + 2):
                        dve.wait_ge(b_mm, 2 * q + 2)
                        if q > 1:
                            dve.wait_ge(b_v, q - 1)
                        n = (q % 2) * 2
                        dve.tensor_tensor(bqkv[:, n:n + 2], ps[:, 2 * n:2 * n + 2, 0:BCOLS],
                                          bb[:].unsqueeze(1).broadcast_to([P, 2, BCOLS]), ALU.add).then_inc(b_qkv, 1)
                    for q in range(2 * b, 2 * b + 2):
                        dve.wait_ge(b_qkv, q + 1)
                        if q > 0:
                            dve.wait_ge(b_rot, q)
                        for n in range(2):
                            for c, (at, w) in enumerate(((0, QW), (QW, KW))):
                                heads = lambda v: v.rearrange("p (h u d) -> p h u d", u=2, d=BD // 2)
                                tile = (q % 2) * 2 + n
                                dve.tensor_tensor(heads(bt2[:, 2 * at + n * w:2 * at + (n + 1) * w]),
                                                  heads(bqkv[:, tile, at:at + w])[:, :, ::-1],
                                                  bsin[:, tile, c:c + 1].rearrange("p o (u d) -> p o u d", u=2)
                                                  .broadcast_to([P, w // BD, 2, BD // 2]), ALU.mult).then_inc(b_sinp, 1)
                        dve.wait_ge(b_cosp, 4 * (q + 1))
                        dve.wait_ge(b_sinp, 4 * (q + 1))
                        if q > 0:
                            dve.wait_ge(b_step, 3 * q)
                        dve.tensor_tensor(brot, bt1, bt2, ALU.add).then_inc(b_rot, 1)
                        dve.wait_ge(b_rot, q + 1)
                        if q > 0:
                            dve.wait_ge(b_stack, 6 * q)
                        dve.tensor_copy(bp1, brot).then_inc(b_step, 1)
                        dve.wait_ge(b_step, 3 * q + 1)
                        dve.tensor_tensor(br1, brot, bp1, ALU.subtract).then_inc(b_step, 1)
                        dve.wait_ge(b_step, 3 * q + 2)
                        dve.tensor_copy(bp2, br1).then_inc(b_step, 1)
                        dve.wait_ge(b_step, 3 * q + 3)
                        dve.tensor_tensor(bp3, br1, bp2, ALU.subtract).then_inc(b_parts, 1)
                        if q > 0:
                            dve.wait_ge(b_turned, 2 * q)
                        for part, v in enumerate((bp1, bp2, bp3)):
                            w = 3 if part < 2 else 2
                            if part == 2:
                                dve.wait_ge(b_parts, q + 1)
                            qv = v[:, 0:2 * QW].rearrange("p (h d) -> p h d", d=BD).unsqueeze(2)
                            kv = v[:, 2 * QW:].rearrange("p (h d) -> p h d", d=BD).unsqueeze(2)
                            dve.tensor_copy(bqs[:].rearrange("p n h c d -> p (n h) c d")[:, :, 3 * part:3 * part + w],
                                            qv.broadcast_to([P, 2 * BH, w, BD])).then_inc(b_stack, 1)
                            dve.tensor_copy(bks[:].rearrange("p n h c d -> p (n h) c d")[:, :, part::3],
                                            kv.broadcast_to([P, 2 * BKV, w, BD])).then_inc(b_stack, 1)
                    small_steps(dve, b, step)
                    for n in range(ST):
                        dve.wait_ge(b_wo, b * ST + n + 1)
                        at = b * ST + n
                        dve.tensor_tensor(x[:, at], x[:, at], ps[:, n % 2, 0:D], ALU.add).then_inc(x_added, 1)

            def experts(l):
                layernorm(2 * l + 1)
                done = l * ROUTE
                def link(op):
                    nonlocal done
                    done += 1
                    op.then_inc(route, 1)
                def linked():
                    dve.wait_ge(route, done)
                over_e = lambda a: a.unsqueeze(2).broadcast_to([P, NT, E])
                bank = ps[:, 4, :].rearrange("p (n e) -> p n e", e=E)
                dve.wait_ge(r_mm, l + 1)
                link(dve.tensor_reduce(rmax[:], bank, AX, ALU.max))
                if l == 0:
                    dve.wait_ge(ld_sh, 12 * 16)
                link(dve.tensor_tensor(lb[:], bank, rbias[:].unsqueeze(1).broadcast_to([P, NT, E]), ALU.add))
                linked()
                dve.tensor_tensor(lg[:], bank, over_e(rmax[:]), ALU.subtract).then_inc(shifted, 1)
                for n in range(NT):
                    link(dve.max(top[:, n], lb[:, n]))
                linked()
                for n in range(NT):
                    link(dve.max_index(topi[:, n], top[:, n], lb[:, n]))
                linked()
                link(dve.tensor_copy(expert[:], topi[:, :, 0:TOPK].rearrange("p n j -> p j n")))
                linked()
                link(dve.tensor_tensor(hot[:], iota[:].unsqueeze(1).unsqueeze(1).broadcast_to([P, TOPK, NT, E]),
                                       expert[:].unsqueeze(3).broadcast_to([P, TOPK, NT, E]), ALU.is_equal))
                linked()
                link(dve.tensor_tensor(prod[:, 0:2], hot[:, 0:2], hot[:, 2:4], ALU.add))
                linked()
                dve.tensor_tensor(chosen[:], prod[:, 0], prod[:, 1], ALU.add).then_inc(chosen_done, 1)
                dve.wait_ge(ex_done, l + 1)
                link(dve.tensor_reduce(rz[:, 0], ex[:], AX, ALU.add))
                linked()
                link(dve.reciprocal(rz[:, 1], rz[:, 0]))
                linked()
                link(dve.tensor_tensor(ex[:], ex[:], over_e(rz[:, 1]), ALU.mult))
                dve.wait_ge(chosen_done, l + 1)
                dve.wait_ge(pos_mm, l + 1)
                ahead = ps[:, 5, :].rearrange("p (n e) -> p n e", e=E)
                dve.scalar_tensor_tensor(out=count[:], in0=chosen[:], scalar=-FAR, in1=ahead, op0=ALU.mult,
                                         op1=ALU.add).then_inc(counted, 1)
                dve.wait_ge(counted, l + 1)
                for n in range(NT):
                    if n >= 3:
                        dve.wait_ge(mark_used, l * NT + n - 2)
                    dve.tensor_tensor(mark[n % 3], count[:, n].unsqueeze(2).broadcast_to([P, E, CAP]),
                                      near[:].unsqueeze(1).broadcast_to([P, E, CAP]), ALU.is_equal).then_inc(marked, 1)
                dve.wait_ge(mark_used, (l + 1) * NT)
                found = ps[:, 4, 0:2 * GROUPS].rearrange("p (g c) -> p g c", c=2)
                dve.tensor_copy(found_row[:], found[:, :, 1]).then_inc(row_found, 1)
                dve.wait_ge(row_found, l + 1)
                dve.scalar_tensor_tensor(out=token_of[:], in0=found[:, :, 0], scalar=float(P), in1=found_row[:],
                                         op0=ALU.mult, op1=ALU.add).then_inc(tokens_ready, 1)
                for it in range(1, GROUPS + 3):
                    if it <= GROUPS:
                        g, u = it - 1, l * GROUPS + it - 1
                        dve.wait_ge(gact_done, u + 1)
                        if g >= 2:
                            dve.wait_ge(hg_turned, u - 1)
                        for c in range(2):
                            dve.scalar_tensor_tensor(out=hg[:, g % 2, c], in0=gact[:, g % 2], scalar=parity[:, c:c + 1],
                                                     in1=ps[:, 2 + g % 2, F:2 * F], op0=ALU.mult, op1=ALU.mult).then_inc(hg_done, 1)
                    if it >= 3:
                        g, u = it - 3, l * GROUPS + it - 3
                        dve.wait_ge(dn_mm, u + 1)
                        if g >= 2 or l > 0:
                            dve.wait_ge(y_out[g % 2], (u // 2) * 16)
                        dve.tensor_copy(yg[:, g % 2], ps[:, 6 + g % 2, 0:D]).then_inc(yg_done, 1)
                    j, piece = (it - 1) // 4, (it - 1) % 4
                    if it <= 4 * TOPK:
                        linked()
                        if piece == 0:
                            link(dve.tensor_tensor(prod[:, j], hot[:, j], ex[:], ALU.mult))
                        elif piece == 1:
                            link(dve.tensor_reduce(score[:, j], prod[:, j], AX, ALU.add))
                        elif piece == 2:
                            link(dve.tensor_tensor(prod[:, j], hot[:, j], ahead, ALU.mult))
                        else:
                            link(dve.tensor_reduce(place[:, j], prod[:, j], AX, ALU.add))
                    elif it == 4 * TOPK + 1:
                        linked()
                        link(dve.tensor_scalar(slot[:], place[:], float(CAP - 1), None, ALU.min))
                        link(dve.tensor_scalar(kept[:], place[:], float(CAP), None, ALU.is_lt))
                        link(dve.tensor_reduce(rz[:, 0], score[:].rearrange("p j n -> p n j"), AX, ALU.add))
                        linked()
                        dve.scalar_tensor_tensor(out=slot_of[:], in0=expert[:], scalar=float(CAP), in1=slot[:],
                                                 op0=ALU.mult, op1=ALU.add).then_inc(slots_ready, 1)
                        link(dve.reciprocal(rz[:, 1], rz[:, 0]))
                        link(dve.tensor_tensor(score[:], score[:], kept[:], ALU.mult))
                        linked()
                        link(dve.tensor_tensor(share[:], score[:], rz[:, 1].unsqueeze(1).broadcast_to([P, TOPK, NT]), ALU.mult))
                linked()
                assert done == (l + 1) * ROUTE, done
                for n in range(NT):
                    dve.wait_ge(sd_mm, l * NT + n + 1)
                    dve.tensor_tensor(x[:, n], x[:, n], ps[:, n % 2, 0:D], ALU.add).then_inc(sd_add, 1)
                    dve.wait_ge(rows_in[n % 2], (l * NT // 2 + n // 2 + 1) * TOPK * 16)
                    dve.wait_ge(sd_add, l * NT + n + 1)
                    for j in range(TOPK):
                        if j > 0:
                            dve.wait_ge(mixed, (l * NT + n) * (TOPK - 1) + j)
                        dve.scalar_tensor_tensor(out=x[:, n], in0=gath[:, n % 2, j], scalar=share[:, j, n:n + 1],
                                                 in1=x[:, n], op0=ALU.mult, op1=ALU.add) \
                            .then_inc(mixed if j < TOPK - 1 else x_added, 1)

            experts(0)
            small_heads()
            experts(1)

        @block.tensor
        def _(pe):
            def turn_xn(r):
                if r == 0:
                    pe.wait_ge(ld_const, 6 * 16)
                for n in range(NT):
                    pe.wait_ge(xn_ready, r * NT + n + 1)
                    for k in range(KT):
                        at = (n % 2 * KT + k) * P
                        mm = pe.transpose(ps[:, n // 2, at:at + P], xn[:, n, k * P:(k + 1) * P], ident[:])
                    mm.then_inc(xn_turned, 1)

            turn_xn(0)
            for c in range(2):
                pe.wait_ge(tab_step, 6 + 5 * c)
                for n in range(ST):
                    mm = pe.transpose(ps[:, 4 + c, n * P:(n + 1) * P], gate[:, 0, 0, n], ident[:])
                mm.then_inc(tab_turned, 1)
            pe.wait_ge(xnT_ready, NT // 2)
            pe.wait_ge(tab_ready, 2)

            def project(dst, s, r, i, a, b):
                st, n = (r // ST) % 2, r % ST
                col = st * S + n * P
                for k in range(KT):
                    if i is None:
                        w = wq[:, (r // 8) % 2, k, a:b]
                    else:
                        w = wq[:, ds((i + r // 8) % 2, 1), k, a:b].rearrange("p a b -> p (a b)")
                    mm = pe.matmul(dst, xnT[:, k, col:col + P], w, start=(k == 0), stop=(k == KT - 1))
                return mm

            def step(s, r, i=None):
                J = REP + 1
                if 1 <= r <= TILES:
                    pe.wait_ge(rope_done, s)
                    pe.wait_ge(gate_done, s)
                    if r >= 2:
                        pe.wait_ge(qkT_done, 2 * s - 2)
                    for h in range(REP):
                        pe.transpose(ps[:, 3, h * P:(h + 1) * P], mb[:, h], ident[:])
                    pe.transpose(ps[:, 2, 0:P], mb[:, REP], ident[:]).then_inc(qk_turned, 1)
                if r < TILES:
                    if r % 8 == 0:
                        g = group_of(r, i)
                        if i is None:
                            pe.wait_ge(ld_wq[g % 2], 16 * (g // 2 + 1))
                        else:
                            pe.wait_ge(ld_wq[1], 16 * ((i + 2) // 2))
                            pe.wait_ge(ld_wq[0], 16 * ((i + 3) // 2))
                    project(ps[:, 0, :], s, r, i, 0, QC).then_inc(q_mm, 1)
                    if r >= 1:
                        pe.wait_ge(v_done, s)
                    project(ps[:, 1, 0:2 * KC], s, r, i, QC, QC + 2 * KC).then_inc(kv_mm, 1)
                if r >= REP and r < LAST - 1:
                    k4 = r - REP
                    st, h = (k4 // REP) % 2, k4 % REP
                    if h == 0:
                        pe.wait_ge(qkT_done, 2 * s)
                    for bank, tiles in enumerate(IN_BANK):
                        if r >= REP + 1:
                            pe.wait_ge(pT_done, (s - REP - 1) * 3 + bank + 1)
                        for i4 in tiles:
                            at = SCORE_AT[i4]
                            pe.matmul(wide[:, at:at + (i4 + 1) * P], qT[:, st, h, i4 * P:(i4 + 1) * P],
                                      kT[:, st, 0:(i4 + 1) * P], start=True, stop=False)
                            mm = pe.matmul(wide[:, at + i4 * P:at + (i4 + 1) * P], identb[:], maskb[:], start=False,
                                           stop=True)
                        mm.then_inc(s_mm, 1)
                if r >= REP + 1:
                    k5 = r - REP - 1
                    st = (k5 // REP) % 2
                    pe.wait_ge(pT_done, (s - REP) * 3)
                    if r >= REP + 2:
                        pe.wait_ge(oT_done, s - REP - 1)
                    for i4 in range(ST):
                        for j in range(i4 + 1):
                            at = TURNED_AT[j] + (i4 - j) * P
                            mm = pe.matmul(ps[:, 7, i4 * HD:(i4 + 1) * HD], pT[:, at:at + P], vA[:, st, j],
                                           start=(j == 0), stop=(j == i4))
                    mm.then_inc(pv_mm, 1)
                if r < TILES:
                    if r >= 1:
                        pe.wait_ge(qkT_done, 2 * s)
                    project(ps[:, 2, :], s, r, i, QC + 2 * KC, COLS).then_inc(gate_mm, 1)
                if r >= REP and r < LAST - 1:
                    pe.wait_ge(exp_done, (s - REP + 1) * NB)
                    for i4 in range(ST):
                        for j in range(i4 + 1):
                            src = SCORE_AT[i4] + j * P
                            at = TURNED_AT[j] + (i4 - j) * P
                            mm = pe.transpose(wide[:, at:at + P], probs[:, src:src + P], ident[:])
                    mm.then_inc(p_turned, 1)
                if r >= REP + 1:
                    pe.wait_ge(o_done, (s - REP) * ST)
                    for i4 in range(ST):
                        mm = pe.transpose(ps[:, 7, i4 * P:(i4 + 1) * P], oA[:, i4], ident[:])
                    mm.then_inc(o_turned, 1)

            steps(pe, step)

            pe.wait_ge(oT_done, HEADS)
            pe.wait_ge(ld_wo, 16)
            for n in range(NT):
                if n >= 4:
                    pe.wait_ge(x_added, n - 3)
                for h in range(H):
                    mm = pe.matmul(ps[:, n % 4, 0:D], oT[:, h, n // ST, (n % ST) * P:(n % ST + 1) * P], wo[:, h],
                                   start=(h == 0), stop=(h == H - 1))
                mm.then_inc(wo_mm, 1)

            def small_heads():
                turn_xn(2)
                pe.wait_ge(xnT_ready, 3 * NT // 2)
                pe.wait_ge(ld_bw, 2 * 16)

                def step(s, r, i=None):
                    if r < BH:
                        banks = bank_set(r)
                        for bank, tiles in enumerate(IN_BANK):
                            if r >= 2:
                                pe.wait_ge(b_pT, (s - 2) * 3 + bank + 1)
                            for i4 in tiles:
                                at = SCORE_AT[i4]
                                if i is None:
                                    q, k = bqT[:, r, i4 * P:(i4 + 1) * P], bkT[:, r // 4, 0:(i4 + 1) * P]
                                else:
                                    q = bqT[:, ds(i * 4 + r, 1), i4 * P:(i4 + 1) * P].rearrange("p a b -> p (a b)")
                                    k = bkT[:, ds(i + r // 4, 1), 0:(i4 + 1) * P].rearrange("p a b -> p (a b)")
                                pe.matmul(banks[:, at:at + (i4 + 1) * P], q, k, start=True, stop=False)
                                mm = pe.matmul(banks[:, at + i4 * P:at + (i4 + 1) * P], identb[:], maskb[:], start=False, stop=True)
                            mm.then_inc(b_s, 1)
                    if r >= 5 and (r - 2) % 4 == 3:
                        g = key_head(r - 5, i)
                        pe.wait_ge(b_pT, (s - 1) * 3)
                        pe.wait_ge(b_vc, g + (b * BKV + 1))
                        if r > 5 or b > 0:
                            pe.wait_ge(b_oT, g + b * BKV)
                        for j in range(ST):
                            for h in range(4):
                                at, w = TURNED_AT[j], S - j * P
                                mm = pe.matmul(ps[h * 32:(h + 1) * 32, 3, j * P:S], bvc[:, j], bpT[:, h, at:at + w],
                                               start=(j == 0), stop=(j == ST - 1))
                        mm.then_inc(b_pv, 1)
                    if 1 <= r <= BH:
                        pe.wait_ge(b_norm, s * ST)
                        banks = bank_set(r - 1)
                        for i4 in range(ST):
                            for j in range(i4 + 1):
                                src = SCORE_AT[i4] + j * P
                                at = TURNED_AT[j] + (i4 - j) * P
                                mm = pe.transpose(banks[:, at:at + P], bp[:, (r - 1) % 2, src:src + P], ident[:])
                        mm.then_inc(b_pturned, 1)

                for b in range(B):
                    if b > 0:
                        pe.wait_ge(x_added, 2 * NT + ST * b)
                    for n in range(ST):
                        m = b * ST + n
                        for k in range(KT):
                            mm = pe.matmul(ps[:, n + n // 2 * 2, 0:BCOLS], xnT[:, k, m * P:(m + 1) * P], wb[:, k],
                                           start=(k == 0), stop=(k == KT - 1))
                        mm.then_inc(b_mm, 1)
                    for n in range(ST):
                        m = b * ST + n
                        banks = TURN_BANKS[n % 2]
                        pe.wait_ge(b_stack, 6 * (m // 2 + 1))
                        if n >= 2:
                            pe.wait_ge(b_qkT, 3 * (m - 1))
                        for h in range(BH):
                            pe.transpose(ps[:, banks[h // 8], :].bitcast(BF16)[:, (h % 8) * P:(h % 8 + 1) * P],
                                         bqs[:, n % 2, h].rearrange("p a b -> p (a b)"), identb[:])
                        for h in range(BKV):
                            mm = pe.transpose(ps[:, banks[2], :].bitcast(BF16)[:, h * P:(h + 1) * P],
                                              bks[:, n % 2, h].rearrange("p a b -> p (a b)"), identb[:])
                        mm.then_inc(b_turned, 1)
                    pe.wait_ge(b_qkT, 3 * (b + 1) * ST)
                    small_steps(pe, b, step)
                    pe.wait_ge(b_oT, (b + 1) * BKV)
                    for n in range(ST):
                        if n >= 2:
                            pe.wait_ge(x_added, 2 * NT + b * ST + n - 1)
                        for g in range(BKV):
                            mm = pe.matmul(ps[:, n % 2, 0:D], boT[:, g, n * P:(n + 1) * P], wob[:, g],
                                           start=(g == 0), stop=(g == BKV - 1))
                        mm.then_inc(b_wo, 1)

            def experts(l):
                turn_xn(2 * l + 1)
                pe.wait_ge(xnT_ready, (2 * l + 2) * NT // 2)
                if l == 0:
                    pe.wait_ge(ld_sh, 12 * 16)
                for n in range(NT):
                    for k in range(KT):
                        mm = pe.matmul(ps[:, 4, n * E:(n + 1) * E], xnT[:, k, n * P:(n + 1) * P], wr[:, k],
                                       start=(k == 0), stop=(k == KT - 1))
                mm.then_inc(r_mm, 1)
                tile = 0
                for c in range(8):
                    if c == 3:
                        pe.wait_ge(chosen_done, l + 1)
                        pe.matmul(ps[:, 5, :], tri[:], chosen[:].rearrange("p n e -> p (n e)"), start=True, stop=False)
                        for d in range(1, NT):
                            mm = pe.matmul(ps[:, 5, d * E:], ones[:], chosen[:, 0:NT - d].rearrange("p n e -> p (n e)"),
                                           start=False, stop=(d == NT - 1))
                        mm.then_inc(pos_mm, 1)
                    if c >= 2:
                        pe.wait_ge(sh_up, l * 8 + c - 1)
                    for bank, w in ((c % 2, wsg), (2 + c % 2, wsu)):
                        for k in range(KT):
                            mm = pe.matmul(ps[:, bank, :], w[:, k, (c % FT) * P:(c % FT + 1) * P],
                                           xnT[:, k, (c // FT) * S:(c // FT + 1) * S], start=(k == 0), stop=(k == KT - 1))
                        mm.then_inc(sh_mm, 1)
                    while tile < MARKED_BY[c]:
                        pe.wait_ge(marked, l * NT + tile + 1)
                        if tile == 0:
                            pe.matmul(ps[:, 4, 0:2 * GROUPS], identb[:], nought[:], start=True, stop=False)
                        for g in range(GROUPS):
                            mm = pe.matmul(ps[:, 4, 2 * g:2 * g + 2], mark[tile % 3][:, g * EG:(g + 1) * EG, :].rearrange("p e c -> p (e c)"),
                                           number[:, tile], start=False, stop=(tile == NT - 1 and g == GROUPS - 1))
                        mm.then_inc(mark_used, 1)
                        tile += 1
                if l == 0:
                    pe.wait_ge(ld_gu, 16)
                    pe.wait_ge(ld_dn, 16)
                pe.wait_ge(sh_up, (l + 1) * 8)
                pe.wait_ge(tokens_ready, l + 1)
                for it in range(GROUPS + 3):
                    if it < GROUPS:
                        g = it
                        pe.wait_ge(xg_in[g], (l + 1) * 16)
                        for k in range(KT):
                            mm = pe.transpose(ps[:, g % 2, k * P:(k + 1) * P], xg[:, g, k * P:(k + 1) * P], ident[:])
                        mm.then_inc(xg_turned, 1)
                    if 1 <= it <= GROUPS:
                        g, u = it - 1, l * GROUPS + it - 1
                        pe.wait_ge(xgT_done, u + 1)
                        if g >= 2:
                            pe.wait_ge(hg_done, 2 * u - 2)
                        for k in range(KT):
                            for e in range(EG):
                                mm = pe.matmul(ps[e * CAP:(e + 1) * CAP, 2 + g % 2, 0:2 * F], xgT[:, g % 2, k, e * CAP:(e + 1) * CAP],
                                               wgu[:, k, g * EG + e], start=(k == 0), stop=(k == KT - 1))
                        mm.then_inc(gu_mm, 1)
                    if 2 <= it <= GROUPS + 1:
                        g, u = it - 2, l * GROUPS + it - 2
                        pe.wait_ge(hg_done, 2 * u + 2)
                        if g >= 1:
                            pe.wait_ge(hgT_done, u)
                        pe.transpose(ps[:, 4, 0:P], hg[:, g % 2].rearrange("p c f -> p (c f)"), ident[:]).then_inc(hg_turned, 1)
                    if it >= 3:
                        g, u = it - 3, l * GROUPS + it - 3
                        pe.wait_ge(hgT_done, u + 1)
                        if g >= 2:
                            pe.wait_ge(yg_done, u - 1)
                        for e in range(EG):
                            mm = pe.matmul(ps[e * CAP:(e + 1) * CAP, 6 + g % 2, 0:D], hgT[:, g % 2, e * CAP:(e + 1) * CAP],
                                           wd[:, (g * EG + e) // 2], start=True, stop=True)
                        mm.then_inc(dn_mm, 1)
                pe.wait_ge(sh_h, (l + 1) * 8)
                for n in range(NT):
                    if n >= 2:
                        pe.wait_ge(sd_add, l * NT + n - 1)
                    for f in range(FT):
                        mm = pe.matmul(ps[:, n % 2, 0:D], hsh[:, f, n * P:(n + 1) * P], wsd[:, f],
                                       start=(f == 0), stop=(f == FT - 1))
                    mm.then_inc(sd_mm, 1)

            experts(0)
            small_heads()
            experts(1)


def constants():
    f = np.float32
    inv = f(1) / (f(1e6) ** (np.arange(0, HD, 2, dtype=f) / f(HD)))
    ang = np.outer(np.arange(S, dtype=f), inv).astype(f)
    c, s = np.cos(ang).astype(f), np.sin(ang).astype(f)
    by_tile = lambda a: np.ascontiguousarray(a.reshape(ST, P, -1).transpose(1, 0, 2))
    bf = mybir.dt.np(BF16)
    mask = np.where(np.arange(P)[None, :] > np.arange(P)[:, None], f(-3e38), f(0))
    row = np.arange(P)
    inv = f(1) / (f(1e6) ** (np.arange(BD // 2, dtype=f) / f(BD // 2)))
    ang = np.outer(np.arange(S, dtype=f), inv).astype(f)
    bc, bs = np.cos(ang).astype(f), np.sin(ang).astype(f)
    for_both = lambda a: np.stack([by_tile(a * f(BD ** -0.5)), by_tile(a)], 2)
    return {
        "b_cos": for_both(np.concatenate([bc, bc], 1)),
        "b_sin": for_both(np.concatenate([-bs, bs], 1)),
        "iota": np.tile(np.arange(E, dtype=f), (P, 1)),
        "nought": np.zeros((P, 2 * GROUPS)).astype(bf),
        "near": np.tile(np.arange(CAP, dtype=f) - f(FAR), (P, 1)),
        "number": np.stack([np.tile(np.arange(NT), (P, 1)), np.tile(row[:, None], (1, NT))], 2).astype(f).astype(bf),
        "parity": np.stack([row // CAP % 2 == 0, row // CAP % 2 == 1], 1).astype(f),
        "tri": (row[:, None] < row[None, :]).astype(bf),
        "ones": np.ones((P, P)).astype(bf),
        "ident": np.eye(P, dtype=f),
        "identb": np.eye(P).astype(bf),
        "maskb": mask.astype(bf),
        "cosf": by_tile(np.concatenate([c, c], 1)),
        "sinf": by_tile(np.concatenate([-s, s], 1)),
    }


def laid_out(i):
    apart = np.concatenate([np.arange(0, HD, 2), np.arange(1, HD, 2)])
    w = np.asarray(i["L0_attn_a_w_qkv"])
    q = w[:H * HD].reshape(KV, REP, HD, D)[:, :, apart].reshape(KV, QC, D)
    gate = w[H * HD:2 * H * HD].reshape(KV, QC, D)
    k = w[2 * H * HD:2 * H * HD + KV * HD].reshape(KV, HD, D)[:, apart]
    v = w[2 * H * HD + KV * HD:].reshape(KV, HD, D)
    w = np.concatenate([q, k, v, gate], 1)
    rows = lambda a: np.broadcast_to(np.asarray(a)[None], (P,) + np.asarray(a).shape)
    vec = np.stack([np.asarray(i[f"L0_attn_a_{n}"])[apart] for n in ("q_norm_w", "q_norm_b", "k_norm_w", "k_norm_b")])
    g = lambda n: np.asarray(i["L0_ffn_" + n])
    shared = lambda a: a.reshape(SF, KT, P).transpose(2, 1, 0)
    bw = [np.asarray(i["L0_attn_b_" + n]) for n in ("Wq", "Wk", "Wv", "bq", "bk", "bv", "Wo")]
    wo_b = bw[6].reshape(BKV, 4, BD, D)
    wo_b = np.concatenate([wo_b, np.zeros_like(wo_b)], 2).reshape(BKV, P, D)
    return {
        "w_bqkv": np.concatenate(bw[0:3], 1).reshape(KT, P, BCOLS).transpose(1, 0, 2),
        "b_bias": rows(np.concatenate(bw[3:6])),
        "w_bo": wo_b.transpose(1, 0, 2),
        "w_sgate": shared(g("sh_gate_w")),
        "w_sup": shared(g("sh_up_w")),
        "w_sdown": g("sh_down_w").transpose(0, 2, 1).reshape(FT, P, D).transpose(1, 0, 2),
        "w_router": g("router_w").reshape(E, KT, P).transpose(2, 1, 0),
        "rbias": rows(g("router_bias")),
        "w_gateup": np.concatenate([g("gate_w"), g("up_w")], 1).reshape(E, 2 * F, KT, P).transpose(3, 2, 0, 1),
        "w_down": g("down_w").transpose(0, 2, 1).reshape(E // 2, P, D).transpose(1, 0, 2),
        "x": np.asarray(i["L0_attn_a_x"]),
        "w_qkvg": w.reshape(KV, COLS, KT, P).transpose(0, 3, 2, 1),
        "w_o": np.asarray(i["L0_attn_a_w_o"]).T.reshape(H, P, D).transpose(1, 0, 2),
        "nvec": rows(vec),
    }


def kernel(**inputs):
    import concourse.bacc as bacc
    from concourse.bass_utils import run_bass_kernel_spmd

    nc = bacc.Bacc("TRN2", target_bir_lowering=False, num_devices=1)
    arrays = {n: np.ascontiguousarray(a) for n, a in {**laid_out(inputs), **constants()}.items()}
    t = {n: nc.dram_tensor(f"in_{n}", a.shape, mybir.dt.from_np(a.dtype), kind="ExternalInput").ap() for n, a in arrays.items()}
    out = nc.dram_tensor("out_x", (B, S, D), F32, kind="ExternalOutput").ap()
    program(nc, t, out)
    got = run_bass_kernel_spmd(nc, [{f"in_{n}": a for n, a in arrays.items()}], core_ids=[0])
    return got.results[0]["out_x"]
```

```python
from contextlib import ExitStack

import numpy as np

import concourse.bass as bass
from concourse import mybir

F32 = mybir.dt.float32
BF16 = mybir.dt.bfloat16
U32 = mybir.dt.uint32
ACT = mybir.ActivationFunctionType
ALU = mybir.AluOpType
AX = mybir.AxisListType.X
ds = bass.ds

P = 128
B, S, D = 2, 512, 256
N = B * S
NT = N // P
ST = S // P
KT = D // P
LN_EPS, HEAD_EPS = 1e-5, 1e-6

H, KV, HD = 16, 4, 128
REP = H // KV
QC, KC = REP * HD, HD
COLS = QC + 2 * KC
LAG = REP + 1

BH, BKV, BD = 16, 4, 16
BCOLS = (BH + 2 * BKV) * BD
SPLITS = 8

E, TOPK, F, CAP, SF = 64, 4, 64, 32, 512
SLOTS = E * CAP
EG = P // CAP
GROUPS = E // EG
LOW = 16300
ROUTE = 46
FT = SF // P
FAR = 4096.0

SCORE_AT = [2 * S - P, 2 * S, S, 0]
TURNED_AT = [0, S, 2 * S, 2 * S - P]
WIDE = 2 * S + 2 * P
IN_BANK = [[3], [2, 0], [1]]
NB = len(IN_BANK)


def program(nc, t, out):
    with ExitStack() as ctx:
        def sb(name, shape, dt=F32, stack=ctx):
            return stack.enter_context(nc.sbuf_tensor(name, shape, dt))

        def sem(name):
            return ctx.enter_context(nc.semaphore(name))

        ps = ctx.enter_context(nc.psum_tensor("ps", [P, 8, 512], F32))
        wide = ps[:, 4:7, :].rearrange("p a b -> p (a b)")

        x = sb("x_res", [P, NT, D])
        xn = sb("xn", [P, NT, D])
        xnT = sb("xnT", [P, KT, N])
        ident = sb("ident", [P, P])
        identb = sb("identb", [P, P], BF16)
        maskb = sb("maskb", [P, P], BF16)
        half = sb("half", [P, 8])
        ln_st = sb("ln_st", [P, NT, 6])
        ln_mv = sb("ln_mv", [P, NT, 2])
        ln_ve = sb("ln_ve", [P, NT])
        ln_rs = sb("ln_rs", [P, NT])
        sums = sb("sums", [P, 2, ST])
        negmax = sb("negmax", [P, 2, ST])
        rinv = sb("rinv", [P, ST])

        in_a = ExitStack()
        wo = sb("w_o", [P, H, D], F32, in_a)
        oT = sb("oT", [P, H, B, S], F32, in_a)
        wq = sb("w_qkv_a", [P, 2, KT, COLS], F32, in_a)
        wg = sb("w_gate", [P, KT, QC], F32, in_a)
        cosf = sb("cosf", [P, ST, HD], F32, in_a)
        sinf = sb("sinf", [P, ST, HD], F32, in_a)
        nvec = sb("nvec", [P, 4, HD], F32, in_a)
        rotA = sb("rotA", [P, 2, ST, HD], F32, in_a)
        rotB = sb("rotB", [P, 2, ST, HD], F32, in_a)
        biasT = sb("biasT", [P, 2, S], F32, in_a)
        nq = sb("nq", [P, REP + 1, HD], F32, in_a)
        ma = sb("ma", [P, REP + 1, HD], F32, in_a)
        mb = sb("mb", [P, REP + 1, HD], F32, in_a)
        hst = sb("hst", [P, REP + 1, 6], F32, in_a)
        hmv = sb("hmv", [P, REP + 1, 2], F32, in_a)
        hve = sb("hve", [P, REP + 1], F32, in_a)
        hneg = sb("hneg", [P, REP + 1], F32, in_a)
        hgo = sb("hgo", [P, 1], F32, in_a)
        hrs = sb("hrs", [P, REP + 1], F32, in_a)
        hnm = sb("hnm", [P, REP + 1], F32, in_a)
        qT = sb("qT", [P, 2, REP, S], F32, in_a)
        kT = sb("kT", [P, 2, S], F32, in_a)
        vA = sb("vA", [P, 2, ST, HD], F32, in_a)
        gate = sb("gate", [P, 2, S], F32, in_a)
        pT = sb("pT", [P, WIDE], F32, in_a)
        probs = sb("probs", [P, WIDE], F32, in_a)

        in_a.close()

        low = ExitStack()
        lg = sb("lg", [P, NT, E], F32, low)
        lb = sb("lb", [P, NT, E], F32, low)
        ex = sb("ex", [P, NT, E], F32, low)
        hot = sb("hot", [P, TOPK, NT, E], F32, low)
        prod = sb("prod", [P, TOPK, NT, E], F32, low)
        chosen = sb("chosen", [P, NT, E], BF16, low)
        top = sb("top", [P, NT, 8], F32, low)
        topi = sb("topi", [P, NT, 8], U32, low)
        rmax = sb("rmax", [P, NT], F32, low)
        rz = sb("rz", [P, 2, NT], F32, low)
        expert = sb("expert", [P, TOPK, NT], F32, low)
        place = sb("place", [P, TOPK, NT], F32, low)
        score = sb("score", [P, TOPK, NT], F32, low)
        share = sb("share", [P, TOPK, NT], F32, low)
        slot = sb("slot", [P, TOPK, NT], F32, low)
        kept = sb("kept", [P, TOPK, NT], F32, low)
        count = lb
        found_row = sb("found_row", [P, GROUPS], F32, low)
        token_of = sb("token_of", [P, GROUPS], U32, low)
        slot_of = sb("slot_of", [P, TOPK, NT], U32, low)
        hsh = sb("hsh", [P, FT, N], F32, low)
        xg = sb("xg", [P, GROUPS, D], F32, low)
        turn = sb("turn", [P, E * CAP // 2], F32, low)
        xgT = turn[:, 0:2 * D].rearrange("p (a k s) -> p a k s", a=2, k=KT)
        yg = turn[:, 2 * D:4 * D].rearrange("p (a d) -> p a d", a=2)
        mark = [v.bitcast(BF16).rearrange("p (e c) -> p e c", c=CAP) for v in (
            prod[:, 0:2].rearrange("p a n e -> p (a n e)"), prod[:, 2:4].rearrange("p a n e -> p (a n e)"),
            turn[:])]
        gact = sb("gact", [P, 2, F], F32, low)
        hg = sb("hg", [P, 2, 2, F], F32, low)
        hgT = sb("hgT", [P, 2, P], F32, low)
        gath = xg[:, 0:2 * TOPK].rearrange("p (a j) d -> p a j d", j=TOPK)
        hup = xg[:].rearrange("p g d -> p (g d)").rearrange("p (c s) -> p c s", s=S)
        low.close()

        low = ExitStack()
        bqs = sb("b_qs", [P, 2, BH, SPLITS, BD], BF16, low)
        bks = sb("b_ks", [P, 2, BKV, SPLITS, BD], BF16, low)
        bqT = sb("b_qT", [P, BH, S], BF16, low)
        bkT = sb("b_kT", [P, BKV, S], BF16, low)
        bv = sb("b_v", [P, ST, BKV, 32], F32, low)
        bvc = sb("b_vc", [P, ST, 32], F32, low)
        bp = sb("b_p", [P, 2, WIDE], F32, low)
        bpT = sb("b_pT", [P, 4, WIDE], F32, low)
        low.close()
        bflat = bpT[:].rearrange("p a b -> p (a b)")
        QW, KW = BH * BD, BKV * BD
        PAIR = 2 * (QW + KW)
        bt1, bt2, brot, br1 = [bflat[:, i * PAIR:(i + 1) * PAIR] for i in range(4)]
        bp1, bp2, bp3 = [bflat[:, 4 * PAIR + i * PAIR // 2:4 * PAIR + (i + 1) * PAIR // 2].bitcast(BF16) for i in range(3)]
        bqkv = bflat[:, 11 * PAIR // 2:11 * PAIR // 2 + ST * BCOLS].rearrange("p (n c) -> p n c", c=BCOLS)
        boT = xn[:].rearrange("p n d -> p (n d)").rearrange("p (k s) -> p k s", s=S)
        sb("low_area", [P, LOW])
        wd = sb("w_down", [P, E // 2, D])
        wsg = sb("w_sgate", [P, KT, SF])
        wsu = sb("w_sup", [P, KT, SF])
        wsd = sb("w_sdown", [P, FT, D])
        wr = sb("w_router", [P, KT, E])
        rbias = sb("rbias", [P, E])
        iota = sb("iota", [P, E])
        near = sb("near", [P, CAP])
        nought = sb("nought", [P, 2 * GROUPS], BF16)
        number = sb("number", [P, NT, 2], BF16)
        parity = sb("parity", [P, 2])
        tri = sb("tri", [P, P], BF16)
        ones = sb("ones", [P, P], BF16)
        wgu = sb("w_gateup", [P, KT, E, 2 * F])

        wb = sb("w_bqkv", [P, KT, BCOLS])
        wob = sb("w_bo", [P, BKV, D])
        bb = sb("b_bias", [P, BCOLS], BF16)
        bcos = sb("b_cos", [P, ST, 2, BD])
        bsin = sb("b_sin", [P, ST, 2, BD])

        xn_dram = nc.dram_tensor("xn_rows", [N, D], F32).ap()
        y_dram = nc.dram_tensor("y_rows", [SLOTS, D], F32).ap()

        ld_x = [sem(f"ld_x{i}") for i in range(2)]
        ld_const = sem("ld_const")
        ld_wq = [sem(f"ld_wq{i}") for i in range(2)]
        ld_wg = sem("ld_wg")
        ld_wo = sem("ld_wo")
        half_ready = sem("half_ready")
        ln_stats = sem("ln_stats")
        ln_aggr = sem("ln_aggr")
        ln_var = sem("ln_var")
        ln_rstd = sem("ln_rstd")
        xn_ready = sem("xn_ready")
        xn_turned = sem("xn_turned")
        xnT_ready = sem("xnT_ready")
        tab_step = sem("tab_step")
        tab_turned = sem("tab_turned")
        tab_ready = sem("tab_ready")
        q_mm = sem("q_mm")
        kv_mm = sem("kv_mm")
        gate_mm = sem("gate_mm")
        gate_done = sem("gate_done")
        v_done = sem("v_done")
        st_step = sem("st_step")
        st_done = sem("st_done")
        head_pow = sem("head_pow")
        head_rs = sem("head_rs")
        norm_done = sem("norm_done")
        rotA_done = sem("rotA_done")
        rotB_done = sem("rotB_done")
        rope_done = sem("rope_done")
        qk_turned = sem("qk_turned")
        qkT_done = sem("qkT_done")
        s_mm = sem("s_mm")
        max_done = sem("max_done")
        exp_done = sem("exp_done")
        p_turned = sem("p_turned")
        pT_done = sem("pT_done")
        pv_mm = sem("pv_mm")
        rinv_done = sem("rinv_done")
        p_normed = sem("p_normed")
        oT_done = sem("oT_done")
        wo_mm = sem("wo_mm")
        x_added = sem("x_added")
        stored = sem("stored")
        ld_sh = sem("ld_sh")
        ld_gu = sem("ld_gu")
        ld_dn = sem("ld_dn")
        xn_out = sem("xn_out")
        counted = sem("counted")
        marked = sem("marked")
        sh_late = sem("sh_late")
        row_found = sem("row_found")
        mark_used = sem("mark_used")
        tokens_ready = sem("tokens_ready")
        r_mm = sem("r_mm")
        route = sem("route")
        shifted = sem("shifted")
        ex_done = sem("ex_done")
        chosen_done = sem("chosen_done")
        pos_mm = sem("pos_mm")
        slots_ready = sem("slots_ready")
        sh_mm = sem("sh_mm")
        sh_act = sem("sh_act")
        sh_up = sem("sh_up")
        sh_h = sem("sh_h")
        sd_mm = sem("sd_mm")
        sd_add = sem("sd_add")
        xg_in = [sem(f"xg_in{g}") for g in range(GROUPS)]
        xg_turned = sem("xg_turned")
        xgT_done = sem("xgT_done")
        gu_mm = sem("gu_mm")
        gact_done = sem("gact_done")
        hg_done = sem("hg_done")
        hg_turned = sem("hg_turned")
        hgT_done = sem("hgT_done")
        dn_mm = sem("dn_mm")
        yg_done = sem("yg_done")
        y_out = [sem(f"y_out{i}") for i in range(2)]
        rows_in = [sem(f"rows_in{i}") for i in range(2)]
        mixed = sem("mixed")
        ld_b = sem("ld_b")
        ld_bw = sem("ld_bw")
        bv_zero = sem("bv_zero")
        b_mm = sem("b_mm")
        b_qkv = sem("b_qkv")
        b_cosp = sem("b_cosp")
        b_sinp = sem("b_sinp")
        b_rot = sem("b_rot")
        b_step = sem("b_step")
        b_parts = sem("b_parts")
        b_v = sem("b_v")
        b_stack = sem("b_stack")
        b_turned = sem("b_turned")
        b_qkT = sem("b_qkT")
        b_s = sem("b_s")
        b_max = sem("b_max")
        b_exp = sem("b_exp")
        b_rinv = sem("b_rinv")
        b_norm = sem("b_norm")
        b_vc = sem("b_vc")
        b_pturned = sem("b_pturned")
        b_pT = sem("b_pT")
        b_pv = sem("b_pv")
        b_oT = sem("b_oT")
        b_wo = sem("b_wo")

        TILES, HEADS = 2 * KV * ST, 2 * KV * REP
        LAST = HEADS + LAG + 1

        def steps(eng, body):
            first = LAG + 2
            for s in range(first):
                body(s, s)
            with eng.Fori(0, KV - 1) as i:
                for c in range(8):
                    body(i * 8 + (first + c), first + c, i)
            for s in range(first + 8 * (KV - 1), LAST):
                body(s, s)

        def small_steps(eng, b, body):
            for u in range(6):
                body(b * BH + u, u)
            with eng.Fori(0, BKV - 2) as i:
                for c in range(4):
                    body(i * 4 + (b * BH + 6 + c), 6 + c, i)
            for u in range(BH - 2, BH + 2):
                body(b * BH + u, u)

        TURN_AT = (0, 4, 4, 4)
        SMALL_OUT = (0, 1, 4, 5)
        TURN_BANKS = ((2, 3, 7), (6, 0, 1))

        EARLY = 6
        MARKED_BY = (0, 0, 0, 1, 3, NT)

        OUT_BANK = (0, 1, 3)

        def first_bank(r):
            return 4 if r < LAG and r % 2 == 1 else 0

        def bank_set(u):
            first = 4 * (u % 2)
            return ps[:, first:first + NB, :].rearrange("p a b -> p (a b)")

        def key_head(r, i):
            return r // 4 if i is None else i + r // 4

        def group_of(r, i):
            return r // 8 if i is None else i + r // 8

        block = ctx.enter_context(nc.Block())

        @block.sync
        def _(sp):
            sp.dma_start(x[:, 0:ST, :], t["x"][0].rearrange("(n p) d -> p n d", p=P)).then_inc(ld_x[0], 16)
            sp.dma_start(x[:, ST:NT, :], t["x"][1].rearrange("(n p) d -> p n d", p=P)).then_inc(ld_x[1], 16)
            sp.dma_start(ident[:], t["ident"]).then_inc(ld_const, 16)
            sp.dma_start(cosf[:], t["cosf"]).then_inc(ld_const, 16)
            sp.dma_start(sinf[:], t["sinf"]).then_inc(ld_const, 16)
            sp.dma_start(nvec[:], t["nvec"]).then_inc(ld_const, 16)
            sp.dma_start(identb[:], t["identb"]).then_inc(ld_const, 16)
            sp.dma_start(maskb[:], t["maskb"]).then_inc(ld_const, 16)
            for g in range(KV):
                if g >= 2:
                    sp.wait_ge(kv_mm, 8 * (g - 1))
                sp.dma_start(wq[:, g % 2], t["w_qkv"][g]).then_inc(ld_wq[g % 2], 16)
                if g >= 2:
                    sp.wait_ge(gate_mm, 8 * (g - 1))
                if g != 1:
                    sp.dma_start(wg[:], t["w_gate"][max(g - 1, 0)]).then_inc(ld_wg, 16)
                if g == 1:
                    sp.dma_start(wo[:], t["w_o"]).then_inc(ld_wo, 16)
            sp.wait_ge(gate_mm, 8 * (KV - 1))
            sp.dma_start(wg[:], t["w_gate"][KV - 1]).then_inc(ld_wg, 16)
            sp.wait_ge(oT_done, HEADS)
            for tile, name in ((wsg, "w_sgate"), (wsu, "w_sup"), (wsd, "w_sdown"), (wr, "w_router"),
                               (rbias, "rbias"), (iota, "iota"), (near, "near"), (number, "number"), (nought, "nought"), (parity, "parity"), (tri, "tri"), (ones, "ones")):
                sp.dma_start(tile[:], t[name]).then_inc(ld_sh, 16)
            sp.dma_start(wgu[:], t["w_gateup"]).then_inc(ld_gu, 16)
            sp.wait_ge(wo_mm, NT)
            sp.dma_start(wd[:], t["w_down"]).then_inc(ld_dn, 16)

            for tile, name in ((bb, "b_bias"), (bcos, "b_cos"), (bsin, "b_sin")):
                sp.dma_start(tile[:], t[name]).then_inc(ld_b, 16)

            def experts(l):
                sp.wait_ge(xn_ready, (2 * l + 2) * NT)
                if l > 0:
                    for g in range(GROUPS):
                        sp.wait_ge(xg_in[g], l * 16)
                sp.dma_start(xn_dram.rearrange("(n p) d -> p n d", p=P), xn[:]).then_inc(xn_out, 16)
                for g in range(GROUPS):
                    sp.wait_ge(yg_done, l * GROUPS + g + 1)
                    sp.dma_start(y_dram[g * P:(g + 1) * P, :], yg[:, g % 2]).then_inc(y_out[g % 2], 16)

            experts(0)
            experts(1)
            for n in range(0, NT, 2):
                sp.wait_ge(x_added, 3 * NT + n + 2)
                sp.dma_start(out.rearrange("b (n p) d -> p (b n) d", p=P)[:, n:n + 2], x[:, n:n + 2]).then_inc(stored, 16)
            sp.wait_ge(stored, NT // 2 * 16)

        @block.gpsimd
        def _(pool):
            pool.memset(half[:], -0.5).then_inc(half_ready, 1)
            pool.wait_ge(half_ready, 1)

            def ln_power(r, b):
                pool.wait_ge(ln_var, 2 * r + b + 1)
                at = slice(b * ST, (b + 1) * ST)
                pool.tensor_tensor(ln_rs[:, at], ln_ve[:, at], half[:, at], ALU.pow).then_inc(ln_rstd, 1)

            for b in range(B):
                ln_power(0, b)

            def step(s, r, i=None):
                if 1 <= r <= TILES:
                    n = (r - 1) % ST
                    pool.wait_ge(norm_done, s * (REP + 1))
                    if r >= 2:
                        pool.wait_ge(rope_done, s - 1)
                    pool.tensor_tensor(ma[:, 0:REP], nq[:, 0:REP], rotA[:, 0, n:n + 1].broadcast_to([P, REP, HD]),
                                       ALU.mult).then_inc(rotA_done, 1)
                    pool.tensor_tensor(ma[:, REP], nq[:, REP], rotA[:, 1, n], ALU.mult).then_inc(rotA_done, 1)
                if r < TILES:
                    pool.wait_ge(st_done, 2 * (s + 1))
                    pool.tensor_tensor(hrs[:], hve[:], half[:, 0:REP + 1], ALU.pow).then_inc(head_pow, 1)
                    pool.wait_ge(head_pow, s + 1)
                    pool.tensor_tensor(hnm[:], hneg[:], hrs[:], ALU.mult).then_inc(head_rs, 1)

            pool.wait_ge(tab_ready, 1)
            steps(pool, step)

            def small_heads():
                pool.memset(bv[:], 0.0).then_inc(bv_zero, 1)
                pool.wait_ge(ld_b, 3 * 16)
                for q in range(NT // 2):
                    pool.wait_ge(b_qkv, q + 1)
                    if q > 0:
                        pool.wait_ge(b_rot, q)
                    for n in range(2):
                        for c, (at, w) in enumerate(((0, QW), (QW, KW))):
                            heads = lambda v: v.rearrange("p (h d) -> p h d", d=BD)
                            tile = (q % 2) * 2 + n
                            pool.tensor_tensor(heads(bt1[:, 2 * at + n * w:2 * at + (n + 1) * w]), heads(bqkv[:, tile, at:at + w]),
                                               bcos[:, tile, c:c + 1].broadcast_to([P, w // BD, BD]), ALU.mult).then_inc(b_cosp, 1)

            def experts(l):
                def hidden(c):
                    pool.wait_ge(sh_act, l * 8 + c + 1)
                    pool.wait_ge(sh_up, l * EARLY + c + 1)
                    at = hsh[:, c % FT, (c // FT) * S:(c // FT + 1) * S]
                    pool.tensor_tensor(at, at, hup[:, c], ALU.mult).then_inc(sh_h, 1)

                for b in range(B):
                    ln_power(2 * l + 1, b)
                if l == 0:
                    pool.wait_ge(wo_mm, NT)
                    pool.dma_start(wb[:], t["w_bqkv"]).then_inc(ld_bw, 16)
                    pool.dma_start(wob[:], t["w_bo"]).then_inc(ld_bw, 16)
                for c in range(EARLY):
                    hidden(c)
                pool.wait_ge(tokens_ready, l + 1)
                pool.wait_ge(xn_out, (l + 1) * 16)
                pool.wait_ge(sh_h, (l + 1) * EARLY)
                for g in range(GROUPS):
                    pool.indirect_dma_start(
                        out=xg[:, g], out_offset=None, in_=xn_dram,
                        in_offset=bass.IndirectOffsetOnAxis(ap=token_of[:, g:g + 1], axis=0),
                        bounds_check=N - 1, oob_is_err=False).then_inc(xg_in[g], 16)
                for i in range(2):
                    pool.wait_ge(y_out[i], (l + 1) * GROUPS // 2 * 16)
                pool.wait_ge(slots_ready, l + 1)
                for n in range(NT):
                    if n >= 2 or l > 0:
                        pool.wait_ge(x_added, 2 * l * NT + NT + n - 1)
                    for j in range(TOPK):
                        pool.indirect_dma_start(
                            out=gath[:, n % 2, j], out_offset=None, in_=y_dram,
                            in_offset=bass.IndirectOffsetOnAxis(ap=slot_of[:, j, n:n + 1], axis=0),
                            bounds_check=SLOTS - 1, oob_is_err=False).then_inc(rows_in[n % 2], 16)
                    if l == 0 and n >= NT - 2:
                        ln_power(2, n - (NT - 2))

            experts(0)
            small_heads()
            experts(1)

        @block.scalar
        def _(act):
            def xnT_copies(r):
                for c in range(NT // 2):
                    act.wait_ge(xn_turned, r * NT + 2 * c + 2)
                    nc.scalar.copy(xnT[:, :, c * 2 * P:(c + 1) * 2 * P].rearrange("p k (n q) -> p n k q", n=2),
                                   ps[:, TURN_AT[r] + c, :].rearrange("p (n k q) -> p n k q", n=2, k=KT)).then_inc(xnT_ready, 1)

            xnT_copies(0)
            for c in range(2):
                act.wait_ge(tab_turned, c + 1)
                nc.scalar.copy(biasT[:, c], ps[:, 4 + c, :]).then_inc(tab_ready, 1)

            def step(s, r, i=None):
                if 1 <= r <= TILES:
                    act.wait_ge(head_rs, s)
                    if r >= 2:
                        act.wait_ge(rope_done, s - 1)
                    bank = first_bank(r - 1)
                    for h in range(REP + 1):
                        src = ps[:, bank, h * HD:(h + 1) * HD] if h < REP else ps[:, bank + 1, 0:HD]
                        nc.scalar.activation(nq[:, h], src, ACT.Identity, bias=hnm[:, h:h + 1],
                                             scale=hrs[:, h:h + 1]).then_inc(norm_done, 1)
                if r >= LAG + 1:
                    act.wait_ge(gate_mm, s - LAG)
                    if r >= LAG + 3:
                        act.wait_ge(oT_done, s - LAG - 2)
                    nc.scalar.activation(gate[:, (r - LAG - 1) % 2], ps[:, 2, :], ACT.Tanh, scale=0.5).then_inc(gate_done, 1)
                if LAG <= r < LAST - 1:
                    kp = (r - LAG) % 2
                    if r >= LAG + 1:
                        act.wait_ge(p_turned, s - LAG)
                    for bank, tiles in enumerate(IN_BANK):
                        act.wait_ge(max_done, (s - LAG) * NB + bank + 1)
                        for i4 in tiles:
                            at = SCORE_AT[i4]
                            op = nc.scalar.activation(probs[:, at:at + (i4 + 1) * P], wide[:, at:at + (i4 + 1) * P],
                                                      ACT.Exp, bias=negmax[:, kp, i4:i4 + 1],
                                                      accum_out=sums[:, kp, i4:i4 + 1])
                        op.then_inc(exp_done, 1)
                if 1 <= r <= TILES:
                    act.wait_ge(kv_mm, s)
                    if r >= LAG + 1:
                        act.wait_ge(pv_mm, s - LAG)
                    nc.scalar.copy(vA[:, ((r - 1) // ST) % 2, (r - 1) % ST],
                                   ps[:, first_bank(r - 1) + 1, KC:2 * KC]).then_inc(v_done, 1)
                if LAG <= r < LAST - 1:
                    act.wait_ge(p_turned, s - LAG + 1)
                    for a, b in ((0, S), (S, 2 * S), (2 * S, WIDE)):
                        nc.scalar.copy(pT[:, a:b], wide[:, a:b]).then_inc(pT_done, 1)

            steps(act, step)

            def small_heads():
                xnT_copies(2)
                act.wait_ge(bv_zero, 1)

                def step(s, r, i=None):
                    kp = r % 2

                    def exponentials(bank):
                        if r >= 2 and bank == 0:
                            act.wait_ge(b_pturned, s - 1)
                        act.wait_ge(b_max, s * NB + bank + 1)
                        for i4 in IN_BANK[bank]:
                            at = SCORE_AT[i4]
                            op = nc.scalar.activation(bp[:, kp, at:at + (i4 + 1) * P], bank_set(r)[:, at:at + (i4 + 1) * P],
                                                      ACT.Exp, bias=negmax[:, kp, i4:i4 + 1],
                                                      accum_out=sums[:, kp, i4:i4 + 1])
                        op.then_inc(b_exp, 1)

                    def turned_copy(bank):
                        if bank == 0:
                            act.wait_ge(b_pturned, s)
                        cols = slice(bank * S, min((bank + 1) * S, WIDE))
                        nc.scalar.copy(bpT[:, (r - 1) % 4, cols], bank_set(r - 1)[:, cols]).then_inc(b_pT, 1)

                    early = 1 <= r < BH and not (r >= 5 and (r - 2) % 4 == 3)
                    for bank in range(NB):
                        if r < BH:
                            exponentials(bank)
                        if early and bank == 1:
                            turned_copy(0)
                    if 1 <= r <= BH:
                        for bank in range(1 if early else 0, NB):
                            turned_copy(bank)
                    if r >= 5 and (r - 2) % 4 == 3:
                        g = key_head(r - 5, i)
                        act.wait_ge(b_pv, g + (b * BKV + 1))
                        dst = boT[:, g] if i is None else boT[:, ds(g, 1)].rearrange("p a b -> p (a b)")
                        nc.scalar.copy(dst, ps[:, 3, :]).then_inc(b_oT, 1)

                for b in range(B):
                    for q in range(2 * b, 2 * b + 2):
                        act.wait_ge(b_qkv, q + 1)
                        n = (q % 2) * 2
                        nc.scalar.copy(bv[:, n:n + 2, :, 0:BD], bqkv[:, n:n + 2, QW + KW:]
                                       .rearrange("p n (h d) -> p n h d", d=BD)).then_inc(b_v, 1)
                    for n in range(ST):
                        act.wait_ge(b_turned, b * ST + n + 1)
                        banks = TURN_BANKS[n % 2]
                        for c in range(2):
                            nc.scalar.copy(bqT[:, 8 * c:8 * c + 8, n * P:(n + 1) * P],
                                           ps[:, banks[c], :].bitcast(BF16).rearrange("p (h q) -> p h q", q=P)).then_inc(b_qkT, 1)
                        nc.scalar.copy(bkT[:, :, n * P:(n + 1) * P],
                                       ps[:, banks[2], 0:2 * P].bitcast(BF16).rearrange("p (h q) -> p h q", q=P)).then_inc(b_qkT, 1)
                    small_steps(act, b, step)

            def experts(l):
                xnT_copies(2 * l + 1)
                act.wait_ge(shifted, l + 1)
                nc.scalar.activation(ex[:], lg[:], ACT.Exp).then_inc(ex_done, 1)
                def hidden_act(c):
                    act.wait_ge(sh_mm, (l * 8 + c + 1) * 2 - 1)
                    nc.scalar.activation(hsh[:, c % FT, (c // FT) * S:(c // FT + 1) * S], ps[:, c % 2, :],
                                         ACT.Silu).then_inc(sh_act, 1)

                for c in range(EARLY):
                    hidden_act(c)
                    act.wait_ge(sh_mm, (l * 8 + c + 1) * 2)
                    if l > 0 and c == 0:
                        act.wait_ge(x_added, (2 * l + 1) * NT)
                    nc.scalar.copy(hup[:, c], ps[:, 2 + c % 2, :]).then_inc(sh_up, 1)
                for it in range(GROUPS + 2):
                    if it < GROUPS:
                        g, u = it, l * GROUPS + it
                        act.wait_ge(xg_turned, u + 1)
                        nc.scalar.copy(xgT[:, g % 2].rearrange("p k s -> p (k s)"),
                                       ps[:, g % 2, 0:KT * P]).then_inc(xgT_done, 1)
                    if 1 <= it <= GROUPS:
                        g, u = it - 1, l * GROUPS + it - 1
                        act.wait_ge(gu_mm, u + 1)
                        if g >= 2:
                            act.wait_ge(hg_done, 2 * u - 2)
                        nc.scalar.activation(gact[:, g % 2], ps[:, 2 + g % 2, 0:F], ACT.Silu).then_inc(gact_done, 1)
                    if it >= 2:
                        g, u = it - 2, l * GROUPS + it - 2
                        act.wait_ge(hg_turned, u + 1)
                        nc.scalar.copy(hgT[:, g % 2], ps[:, 4, 0:P]).then_inc(hgT_done, 1)
                for c in range(EARLY, 8):
                    hidden_act(c)

            experts(0)
            small_heads()
            experts(1)

        @block.vector
        def _(dve):
            def ln_tile(r, n):
                if r > 0:
                    dve.wait_ge(x_added, (r - 1) * NT + n + 1)
                dve.bn_stats(ln_st[:, n], x[:, n]).then_inc(ln_stats, 1)

            def ln_moments(r, b):
                for n in range(b * ST, (b + 1) * ST):
                    dve.wait_ge(ln_stats, r * NT + n + 1)
                    dve.bn_aggr(ln_mv[:, n], ln_st[:, n]).then_inc(ln_aggr, 1)
                dve.wait_ge(ln_aggr, r * NT + (b + 1) * ST)
                at = slice(b * ST, (b + 1) * ST)
                dve.tensor_scalar(ln_ve[:, at], ln_mv[:, at, 1], LN_EPS, None, ALU.add).then_inc(ln_var, 1)

            def ln_apply(r, b):
                dve.wait_ge(ln_rstd, 2 * r + b + 1)
                for n in range(b * ST, (b + 1) * ST):
                    dve.tensor_scalar(xn[:, n], x[:, n], ln_mv[:, n, 0:1], ln_rs[:, n:n + 1], ALU.subtract,
                                      ALU.mult).then_inc(xn_ready, 1)

            def ln_behind(r, n):
                ln_tile(r, n)
                if n % ST == ST - 1:
                    ln_moments(r, n // ST)
                if n == NT - 2 or n == NT - 1:
                    ln_apply(r, n - (NT - 2))

            for b in range(B):
                dve.wait_ge(ld_x[b], 16)
                for n in range(b * ST, (b + 1) * ST):
                    ln_tile(0, n)
                ln_moments(0, b)
            for b in range(B):
                ln_apply(0, b)

            dve.wait_ge(ld_const, 6 * 16)
            dve.tensor_scalar(nvec[:, 0:2], nvec[:, 0:2], HD ** -0.5, None, ALU.mult).then_inc(tab_step, 1)
            dve.wait_ge(tab_step, 1)

            def over_tiles(v, swapped=False):
                v = v.rearrange("p (a b) -> p a b", a=2)
                v = v[:, ::-1, :] if swapped else v
                return v.unsqueeze(1).broadcast_to([P, ST, 2, HD // 2])

            halves = lambda a: a.rearrange("p n (a b) -> p n a b", a=2)
            done = 1
            for c in range(2):
                w, b = nvec[:, 2 * c], nvec[:, 2 * c + 1]
                dve.tensor_tensor(halves(rotA[:, c]), halves(cosf[:]), over_tiles(w), ALU.mult).then_inc(tab_step, 1)
                dve.tensor_tensor(halves(rotB[:, c]), halves(sinf[:]), over_tiles(w, True), ALU.mult).then_inc(tab_step, 1)
                if c == 1:
                    dve.wait_ge(tab_turned, 1)
                ta, tb = [gate[:, n].rearrange("p (n d) -> p n d", d=HD) for n in range(2)]
                dve.tensor_tensor(halves(ta), halves(cosf[:]), over_tiles(b), ALU.mult).then_inc(tab_step, 1)
                dve.tensor_tensor(halves(tb), halves(sinf[:]), over_tiles(b, True), ALU.mult).then_inc(tab_step, 1)
                done += 4
                dve.wait_ge(tab_step, done)
                dve.tensor_tensor(ta, ta, tb, ALU.add).then_inc(tab_step, 1)
                done += 1

            def add_output(n):
                dve.wait_ge(wo_mm, n + 1)
                dve.tensor_tensor(x[:, n], x[:, n], ps[:, OUT_BANK[n % len(OUT_BANK)], 0:D], ALU.add).then_inc(x_added, 1)
                ln_behind(1, n)

            def step(s, r, i=None):
                J = REP + 1

                def rotated():
                    n = (r - 1) % ST
                    dve.wait_ge(norm_done, s * J)
                    if r >= 2:
                        dve.wait_ge(qk_turned, s - 1)
                    swapped = lambda a: a.rearrange("p h (a b) -> p h a b", a=2)[:, :, ::-1, :]
                    plain = lambda a: a.rearrange("p h (a b) -> p h a b", a=2)
                    dve.tensor_tensor(plain(mb[:, 0:REP]), swapped(nq[:, 0:REP]),
                                      plain(rotB[:, 0, n:n + 1]).broadcast_to([P, REP, 2, HD // 2]), ALU.mult).then_inc(rotB_done, 1)
                    dve.tensor_tensor(plain(mb[:, REP:J]), swapped(nq[:, REP:J]), plain(rotB[:, 1, n:n + 1]),
                                      ALU.mult).then_inc(rotB_done, 1)
                    dve.wait_ge(rotA_done, s * 2)
                    dve.wait_ge(rotB_done, s * 2)
                    dve.tensor_tensor(mb[:], ma[:], mb[:], ALU.add).then_inc(rope_done, 1)

                def query_moments():
                    dve.wait_ge(q_mm, s + 1)
                    if r >= 1:
                        dve.wait_ge(st_step, s * 2 * J)
                    for h in range(REP):
                        dve.bn_stats(hst[:, h], ps[:, first_bank(r), h * HD:(h + 1) * HD]).then_inc(st_step, 1)

                def turned():
                    m = r - 1
                    st, n = (m // ST) % 2, m % ST
                    if r == 1:
                        dve.wait_ge(tab_ready, 2)
                    dve.wait_ge(qk_turned, s)
                    dve.tensor_tensor(qT[:, st, :, n * P:(n + 1) * P], ps[:, 3, :].rearrange("p (h q) -> p h q", h=REP),
                                      biasT[:, 0:1, n * P:(n + 1) * P].broadcast_to([P, REP, P]), ALU.add).then_inc(qkT_done, 1)
                    dve.tensor_tensor(kT[:, st, n * P:(n + 1) * P], ps[:, 2, 0:P], biasT[:, 1, n * P:(n + 1) * P],
                                      ALU.add).then_inc(qkT_done, 1)

                def key_moments():
                    dve.wait_ge(kv_mm, s + 1)
                    dve.bn_stats(hst[:, REP], ps[:, first_bank(r) + 1, 0:HD]).then_inc(st_step, 1)
                    dve.wait_ge(st_step, s * 2 * J + J)
                    dve.tensor_copy(hgo[:], hst[:, 0, 0:1])
                    for h in range(J):
                        dve.bn_aggr(hmv[:, h], hst[:, h]).then_inc(st_step, 1)
                    dve.wait_ge(st_step, (s + 1) * 2 * J)
                    if 1 <= r < LAG:
                        dve.wait_ge(head_rs, s)
                    dve.tensor_scalar(hve[:], hmv[:, :, 1], HEAD_EPS, None, ALU.add).then_inc(st_done, 1)
                    dve.tensor_scalar(hneg[:], hmv[:, :, 0], -1.0, None, ALU.mult).then_inc(st_done, 1)

                if r < LAG:
                    query_moments()
                    key_moments()
                    if r >= 1:
                        rotated()
                        turned()
                if LAG <= r < LAST - 1:
                    kp = (r - LAG) % 2
                    for bank, tiles in enumerate(IN_BANK):
                        dve.wait_ge(s_mm, (s - LAG) * NB + bank + 1)
                        for i4 in tiles:
                            at = SCORE_AT[i4]
                            op = dve.tensor_reduce(negmax[:, kp, i4:i4 + 1], wide[:, at:at + (i4 + 1) * P], AX,
                                                   ALU.max, negate=True)
                        op.then_inc(max_done, 1)
                if LAG <= r <= TILES:
                    rotated()
                if LAG <= r < LAST - 1:
                    dve.wait_ge(exp_done, (s - LAG + 1) * NB)
                    if r >= LAG + 1:
                        dve.wait_ge(p_normed, (s - LAG) * ST)
                    dve.reciprocal(rinv[:], sums[:, kp]).then_inc(rinv_done, 1)
                    dve.wait_ge(rinv_done, s - LAG + 1)
                    for i4 in range(ST):
                        at = SCORE_AT[i4]
                        dve.tensor_scalar(probs[:, at:at + (i4 + 1) * P], probs[:, at:at + (i4 + 1) * P],
                                          rinv[:, i4:i4 + 1], 0.5, ALU.mult, ALU.mult).then_inc(p_normed, 1)
                if r >= LAG + 1:
                    k = r - LAG - 1
                    dve.wait_ge(pv_mm, s - LAG)
                    dve.wait_ge(gate_done, s - LAG)
                    g, h = group_of(k, i), k % REP
                    dst = oT[:, g * REP + h, (k // REP) % 2] if i is None else \
                        oT[:, ds(g * REP + h, 1), (k // REP) % 2].rearrange("p a b -> p (a b)")
                    dve.scalar_tensor_tensor(out=dst, in0=gate[:, k % 2], scalar=1.0, in1=ps[:, 7, :], op0=ALU.add,
                                             op1=ALU.mult).then_inc(oT_done, 1)
                if r >= LAST - ST + 1:
                    add_output(r - (LAST - ST + 1))
                if LAG <= r < TILES:
                    query_moments()
                if LAG <= r <= TILES:
                    turned()
                if LAG <= r < TILES:
                    key_moments()

            steps(dve, step)

            for n in range(ST - 1, NT):
                add_output(n)

            def small_heads():
                dve.wait_ge(ld_b, 3 * 16)

                def step(s, r, i=None):
                    if r < BH:
                        banks = bank_set(r)
                        for bank, tiles in enumerate(IN_BANK):
                            dve.wait_ge(b_s, s * NB + bank + 1)
                            for i4 in tiles:
                                at = SCORE_AT[i4]
                                op = dve.tensor_reduce(negmax[:, r % 2, i4:i4 + 1], banks[:, at:at + (i4 + 1) * P], AX,
                                                       ALU.max, negate=True)
                            op.then_inc(b_max, 1)
                    if r < BH:
                        kp = r % 2
                        if r >= 1 or b > 0:
                            dve.wait_ge(b_norm, s * ST)
                        for bank, tiles in enumerate(IN_BANK):
                            dve.wait_ge(b_exp, s * NB + bank + 1)
                            some = slice(min(tiles), max(tiles) + 1, 2)
                            dve.reciprocal(rinv[:, some], sums[:, kp, some]).then_inc(b_rinv, 1)
                            dve.wait_ge(b_rinv, s * NB + bank + 1)
                            for i4 in tiles:
                                at = SCORE_AT[i4]
                                dve.tensor_scalar(bp[:, kp, at:at + (i4 + 1) * P], bp[:, kp, at:at + (i4 + 1) * P],
                                                  rinv[:, i4:i4 + 1], None, ALU.mult).then_inc(b_norm, 1)
                    if r % 4 == 3:
                        g = key_head(r, i)
                        dve.wait_ge(b_v, 2 * b + 2)
                        if r > 3 or b > 0:
                            dve.wait_ge(b_pv, g + b * BKV)
                        src = bv[:, :, g] if i is None else bv[:, :, ds(g, 1)].rearrange("p a b c -> p a (b c)")
                        dve.tensor_copy(bvc[:], src).then_inc(b_vc, 1)

                def add_small(b):
                    for n in range(ST):
                        dve.wait_ge(b_wo, b * ST + n + 1)
                        at = b * ST + n
                        dve.tensor_tensor(x[:, at], x[:, at], ps[:, SMALL_OUT[n], 0:D], ALU.add).then_inc(x_added, 1)
                        ln_tile(3, at)
                    ln_moments(3, b)

                for b in range(B):
                    for q in range(2 * b, 2 * b + 2):
                        dve.wait_ge(b_mm, 2 * q + 2)
                        if q > 1:
                            dve.wait_ge(b_v, q - 1)
                        n = (q % 2) * 2
                        dve.tensor_tensor(bqkv[:, n:n + 2], ps[:, 2 + n:4 + n, 0:BCOLS],
                                          bb[:].unsqueeze(1).broadcast_to([P, 2, BCOLS]), ALU.add).then_inc(b_qkv, 1)
                    for q in range(2 * b, 2 * b + 2):
                        if b > 0 and q % 2 == 1:
                            add_small(b - 1)
                        dve.wait_ge(b_qkv, q + 1)
                        if q > 0:
                            dve.wait_ge(b_rot, q)
                        for n in range(2):
                            for c, (at, w) in enumerate(((0, QW), (QW, KW))):
                                heads = lambda v: v.rearrange("p (h u d) -> p h u d", u=2, d=BD // 2)
                                tile = (q % 2) * 2 + n
                                dve.tensor_tensor(heads(bt2[:, 2 * at + n * w:2 * at + (n + 1) * w]),
                                                  heads(bqkv[:, tile, at:at + w])[:, :, ::-1],
                                                  bsin[:, tile, c:c + 1].rearrange("p o (u d) -> p o u d", u=2)
                                                  .broadcast_to([P, w // BD, 2, BD // 2]), ALU.mult).then_inc(b_sinp, 1)
                        dve.wait_ge(b_cosp, 4 * (q + 1))
                        dve.wait_ge(b_sinp, 4 * (q + 1))
                        if q > 0:
                            dve.wait_ge(b_step, 3 * q)
                        dve.tensor_tensor(brot, bt1, bt2, ALU.add).then_inc(b_rot, 1)
                        dve.wait_ge(b_rot, q + 1)
                        if q > 0:
                            dve.wait_ge(b_stack, 6 * q)
                        dve.tensor_copy(bp1, brot).then_inc(b_step, 1)
                        dve.wait_ge(b_step, 3 * q + 1)
                        dve.tensor_tensor(br1, brot, bp1, ALU.subtract).then_inc(b_step, 1)
                        dve.wait_ge(b_step, 3 * q + 2)
                        dve.tensor_copy(bp2, br1).then_inc(b_step, 1)
                        dve.wait_ge(b_step, 3 * q + 3)
                        dve.tensor_tensor(bp3, br1, bp2, ALU.subtract).then_inc(b_parts, 1)
                        if q > 0:
                            dve.wait_ge(b_turned, 2 * q)
                        for part, v in enumerate((bp1, bp2, bp3)):
                            w = 3 if part < 2 else 2
                            if part == 2:
                                dve.wait_ge(b_parts, q + 1)
                            qv = v[:, 0:2 * QW].rearrange("p (h d) -> p h d", d=BD).unsqueeze(2)
                            kv = v[:, 2 * QW:].rearrange("p (h d) -> p h d", d=BD).unsqueeze(2)
                            dve.tensor_copy(bqs[:].rearrange("p n h c d -> p (n h) c d")[:, :, 3 * part:3 * part + w],
                                            qv.broadcast_to([P, 2 * BH, w, BD])).then_inc(b_stack, 1)
                            dve.tensor_copy(bks[:].rearrange("p n h c d -> p (n h) c d")[:, :, part::3],
                                            kv.broadcast_to([P, 2 * BKV, w, BD])).then_inc(b_stack, 1)
                    small_steps(dve, b, step)
                add_small(B - 1)
                dve.wait_ge(b_wo, B * ST)
                for b in range(B):
                    ln_apply(3, b)

            def experts(l):
                done = l * ROUTE
                def link(op):
                    nonlocal done
                    done += 1
                    op.then_inc(route, 1)
                def linked():
                    dve.wait_ge(route, done)
                over_e = lambda a: a.unsqueeze(2).broadcast_to([P, NT, E])
                bank = ps[:, 4, :].rearrange("p (n e) -> p n e", e=E)
                dve.wait_ge(r_mm, l + 1)
                link(dve.tensor_reduce(rmax[:], bank, AX, ALU.max))
                if l == 0:
                    dve.wait_ge(ld_sh, 12 * 16)
                link(dve.tensor_tensor(lb[:], bank, rbias[:].unsqueeze(1).broadcast_to([P, NT, E]), ALU.add))
                linked()
                dve.tensor_tensor(lg[:], bank, over_e(rmax[:]), ALU.subtract).then_inc(shifted, 1)
                for n in range(NT):
                    link(dve.max(top[:, n], lb[:, n]))
                linked()
                for n in range(NT):
                    link(dve.max_index(topi[:, n], top[:, n], lb[:, n]))
                linked()
                link(dve.tensor_copy(expert[:], topi[:, :, 0:TOPK].rearrange("p n j -> p j n")))
                linked()
                link(dve.tensor_tensor(hot[:], iota[:].unsqueeze(1).unsqueeze(1).broadcast_to([P, TOPK, NT, E]),
                                       expert[:].unsqueeze(3).broadcast_to([P, TOPK, NT, E]), ALU.is_equal))
                linked()
                link(dve.tensor_tensor(prod[:, 0:2], hot[:, 0:2], hot[:, 2:4], ALU.add))
                linked()
                dve.tensor_tensor(chosen[:], prod[:, 0], prod[:, 1], ALU.add).then_inc(chosen_done, 1)
                dve.wait_ge(ex_done, l + 1)
                link(dve.tensor_reduce(rz[:, 0], ex[:], AX, ALU.add))
                linked()
                link(dve.reciprocal(rz[:, 1], rz[:, 0]))
                linked()
                link(dve.tensor_tensor(ex[:], ex[:], over_e(rz[:, 1]), ALU.mult))
                dve.wait_ge(chosen_done, l + 1)
                dve.wait_ge(pos_mm, l + 1)
                ahead = ps[:, 5, :].rearrange("p (n e) -> p n e", e=E)
                dve.scalar_tensor_tensor(out=count[:], in0=chosen[:], scalar=-FAR, in1=ahead, op0=ALU.mult,
                                         op1=ALU.add).then_inc(counted, 1)
                dve.wait_ge(counted, l + 1)
                for n in range(NT):
                    if n >= 3:
                        dve.wait_ge(mark_used, l * NT + n - 2)
                    dve.tensor_tensor(mark[n % 3], count[:, n].unsqueeze(2).broadcast_to([P, E, CAP]),
                                      near[:].unsqueeze(1).broadcast_to([P, E, CAP]), ALU.is_equal).then_inc(marked, 1)
                dve.wait_ge(mark_used, (l + 1) * NT)
                found = ps[:, 4, 0:2 * GROUPS].rearrange("p (g c) -> p g c", c=2)
                dve.tensor_copy(found_row[:], found[:, :, 1]).then_inc(row_found, 1)
                dve.wait_ge(row_found, l + 1)
                dve.scalar_tensor_tensor(out=token_of[:], in0=found[:, :, 0], scalar=float(P), in1=found_row[:],
                                         op0=ALU.mult, op1=ALU.add).then_inc(tokens_ready, 1)
                for it in range(1, GROUPS + 3):
                    if it <= GROUPS:
                        g, u = it - 1, l * GROUPS + it - 1
                        dve.wait_ge(gact_done, u + 1)
                        if g >= 2:
                            dve.wait_ge(hg_turned, u - 1)
                        for c in range(2):
                            dve.scalar_tensor_tensor(out=hg[:, g % 2, c], in0=gact[:, g % 2], scalar=parity[:, c:c + 1],
                                                     in1=ps[:, 2 + g % 2, F:2 * F], op0=ALU.mult, op1=ALU.mult).then_inc(hg_done, 1)
                    if it >= 3:
                        g, u = it - 3, l * GROUPS + it - 3
                        dve.wait_ge(dn_mm, u + 1)
                        if g >= 2 or l > 0:
                            dve.wait_ge(y_out[g % 2], (u // 2) * 16)
                        dve.tensor_copy(yg[:, g % 2], ps[:, 6 + g % 2, 0:D]).then_inc(yg_done, 1)
                    j, piece = (it - 1) // 4, (it - 1) % 4
                    if it <= 4 * TOPK:
                        linked()
                        if piece == 0:
                            link(dve.tensor_tensor(prod[:, j], hot[:, j], ex[:], ALU.mult))
                        elif piece == 1:
                            link(dve.tensor_reduce(score[:, j], prod[:, j], AX, ALU.add))
                        elif piece == 2:
                            link(dve.tensor_tensor(prod[:, j], hot[:, j], ahead, ALU.mult))
                        else:
                            link(dve.tensor_reduce(place[:, j], prod[:, j], AX, ALU.add))
                    elif it == 4 * TOPK + 1:
                        linked()
                        link(dve.tensor_scalar(slot[:], place[:], float(CAP - 1), None, ALU.min))
                        link(dve.tensor_scalar(kept[:], place[:], float(CAP), None, ALU.is_lt))
                        link(dve.tensor_reduce(rz[:, 0], score[:].rearrange("p j n -> p n j"), AX, ALU.add))
                        linked()
                        dve.scalar_tensor_tensor(out=slot_of[:], in0=expert[:], scalar=float(CAP), in1=slot[:],
                                                 op0=ALU.mult, op1=ALU.add).then_inc(slots_ready, 1)
                        link(dve.reciprocal(rz[:, 1], rz[:, 0]))
                        link(dve.tensor_tensor(score[:], score[:], kept[:], ALU.mult))
                        linked()
                        link(dve.tensor_tensor(share[:], score[:], rz[:, 1].unsqueeze(1).broadcast_to([P, TOPK, NT]), ALU.mult))
                linked()
                assert done == (l + 1) * ROUTE, done
                for n in range(NT):
                    dve.wait_ge(sd_mm, l * NT + n + 1)
                    dve.tensor_tensor(x[:, n], x[:, n], ps[:, 4 + n % 4, 0:D], ALU.add).then_inc(sd_add, 1)
                    dve.wait_ge(rows_in[n % 2], (l * NT // 2 + n // 2 + 1) * TOPK * 16)
                    dve.wait_ge(sd_add, l * NT + n + 1)
                    for j in range(TOPK):
                        if j > 0:
                            dve.wait_ge(mixed, (l * NT + n) * (TOPK - 1) + j)
                        dve.scalar_tensor_tensor(out=x[:, n], in0=gath[:, n % 2, j], scalar=share[:, j, n:n + 1],
                                                 in1=x[:, n], op0=ALU.mult, op1=ALU.add) \
                            .then_inc(mixed if j < TOPK - 1 else x_added, 1)
                    if EARLY + n < 8:
                        c = EARLY + n
                        dve.wait_ge(sh_act, l * 8 + c + 1)
                        dve.wait_ge(sh_mm, (l * 8 + c + 1) * 2)
                        at = hsh[:, c % FT, (c // FT) * S:(c // FT + 1) * S]
                        dve.tensor_tensor(at, at, ps[:, 2 + c % 2, :], ALU.mult).then_inc(sh_late, 1)
                    if l == 0:
                        ln_behind(2, n)

            experts(0)
            small_heads()
            experts(1)

        @block.tensor
        def _(pe):
            def turn_xn(r, b):
                for n in range(b * ST, (b + 1) * ST):
                    pe.wait_ge(xn_ready, r * NT + n + 1)
                    for k in range(KT):
                        at = (n % 2 * KT + k) * P
                        mm = pe.transpose(ps[:, TURN_AT[r] + n // 2, at:at + P], xn[:, n, k * P:(k + 1) * P], ident[:])
                    mm.then_inc(xn_turned, 1)

            pe.wait_ge(ld_const, 6 * 16)
            for b in range(B):
                turn_xn(0, b)
            for c in range(2):
                pe.wait_ge(tab_step, 6 + 5 * c)
                for n in range(ST):
                    mm = pe.transpose(ps[:, 4 + c, n * P:(n + 1) * P], gate[:, 0, n * HD:(n + 1) * HD], ident[:])
                mm.then_inc(tab_turned, 1)
            pe.wait_ge(xnT_ready, NT // 2)
            pe.wait_ge(tab_ready, 2)

            def project(dst, s, r, i, a, b):
                st, n = (r // ST) % 2, r % ST
                col = st * S + n * P
                for k in range(KT):
                    if i is None:
                        w = wq[:, (r // 8) % 2, k, a:b]
                    else:
                        w = wq[:, ds((i + r // 8) % 2, 1), k, a:b].rearrange("p a b -> p (a b)")
                    mm = pe.matmul(dst, xnT[:, k, col:col + P], w, start=(k == 0), stop=(k == KT - 1))
                return mm

            def project_out(n):
                if n == 0:
                    pe.wait_ge(ld_wo, 16)
                    pe.wait_ge(oT_done, HEADS - REP)
                if n == ST:
                    pe.wait_ge(oT_done, HEADS)
                if n >= len(OUT_BANK):
                    pe.wait_ge(x_added, n - len(OUT_BANK) + 1)
                for h in range(H):
                    mm = pe.matmul(ps[:, OUT_BANK[n % len(OUT_BANK)], 0:D], oT[:, h, n // ST, (n % ST) * P:(n % ST + 1) * P],
                                   wo[:, h], start=(h == 0), stop=(h == H - 1))
                mm.then_inc(wo_mm, 1)

            def step(s, r, i=None):
                J = REP + 1
                if r == LAST - 1:
                    project_out(ST - 1)
                if LAG <= r < LAST - 1:
                    k = r - LAG
                    st, h = (k // REP) % 2, k % REP
                    if h == 0:
                        pe.wait_ge(qkT_done, 2 * (s - 1))
                    if r == LAG:
                        pe.wait_ge(v_done, s - 1)
                    for bank, tiles in enumerate(IN_BANK):
                        if r >= LAG + 1:
                            pe.wait_ge(pT_done, (s - LAG - 1) * 3 + bank + 1)
                        for i4 in tiles:
                            at = SCORE_AT[i4]
                            pe.matmul(wide[:, at:at + (i4 + 1) * P], qT[:, st, h, i4 * P:(i4 + 1) * P],
                                      kT[:, st, 0:(i4 + 1) * P], start=True, stop=False)
                            mm = pe.matmul(wide[:, at + i4 * P:at + (i4 + 1) * P], identb[:], maskb[:], start=False,
                                           stop=True)
                        mm.then_inc(s_mm, 1)
                if r >= LAG + 1:
                    st = ((r - LAG - 1) // REP) % 2
                    pe.wait_ge(pT_done, (s - LAG) * 3)
                    if r > TILES:
                        pe.wait_ge(v_done, TILES)
                    if r >= LAG + 2:
                        pe.wait_ge(oT_done, s - LAG - 1)
                    for j in range(ST):
                        mm = pe.matmul(ps[:, 7, j * P:S], vA[:, st, j], pT[:, TURNED_AT[j]:TURNED_AT[j] + S - j * P],
                                       start=(j == 0), stop=(j == ST - 1))
                    mm.then_inc(pv_mm, 1)
                if LAST - ST <= r < LAST - 1:
                    project_out(r - (LAST - ST))

                def turn_last():
                    pe.wait_ge(rope_done, s)
                    if r >= 2:
                        pe.wait_ge(qkT_done, 2 * s - 2)
                    if r >= LAG + 1:
                        pe.wait_ge(gate_done, s - LAG)
                    for h in range(REP):
                        pe.transpose(ps[:, 3, h * P:(h + 1) * P], mb[:, h], ident[:])
                    pe.transpose(ps[:, 2, 0:P], mb[:, REP], ident[:]).then_inc(qk_turned, 1)

                def project_queries(s, r):
                    if r % 8 == 0:
                        g = group_of(r, i)
                        if i is None:
                            pe.wait_ge(ld_wq[g % 2], 16 * (g // 2 + 1))
                        else:
                            pe.wait_ge(ld_wq[1], 16 * ((i + 2) // 2))
                            pe.wait_ge(ld_wq[0], 16 * ((i + 3) // 2))
                    if r >= LAG:
                        pe.wait_ge(norm_done, s * J)
                    elif r >= 2:
                        pe.wait_ge(norm_done, (s - 1) * J)
                    project(ps[:, first_bank(r), :], s, r, i, 0, QC).then_inc(q_mm, 1)

                def project_keys(s, r):
                    if r >= LAG:
                        pe.wait_ge(v_done, s)
                    elif r >= 2:
                        pe.wait_ge(v_done, s - 1)
                    project(ps[:, first_bank(r) + 1, 0:2 * KC], s, r, i, QC, QC + 2 * KC).then_inc(kv_mm, 1)

                if r < LAG:
                    for tile in (0, 1) if r == 0 else (r + 1,) if r + 1 < LAG else ():
                        project_queries(tile, tile)
                        project_keys(tile, tile)
                    if r >= 1:
                        turn_last()
                else:
                    if r < TILES:
                        project_queries(s, r)
                    if r <= TILES:
                        turn_last()
                    if r < TILES:
                        project_keys(s, r)
                if LAG <= r < LAST - 1:
                    pe.wait_ge(p_normed, (s - LAG + 1) * ST)
                    for i4 in range(ST):
                        for j in range(i4 + 1):
                            src = SCORE_AT[i4] + j * P
                            at = TURNED_AT[j] + (i4 - j) * P
                            mm = pe.transpose(wide[:, at:at + P], probs[:, src:src + P], ident[:])
                    mm.then_inc(p_turned, 1)
                    k = r - LAG
                    st, h = (k // REP) % 2, k % REP
                    if k % 8 == 0:
                        g = group_of(k, i)
                        pe.wait_ge(ld_wg, 16 * (g + 1))
                    if r <= TILES:
                        pe.wait_ge(qkT_done, 2 * s)
                    if r >= LAG + 1:
                        pe.wait_ge(gate_done, s - LAG)
                    for c in range(KT):
                        mm = pe.matmul(ps[:, 2, :], wg[:, c, h * HD:(h + 1) * HD], xnT[:, c, st * S:(st + 1) * S],
                                       start=(c == 0), stop=(c == KT - 1))
                    mm.then_inc(gate_mm, 1)

            steps(pe, step)

            for n in range(ST, NT):
                project_out(n)
            for b in range(B):
                turn_xn(1, b)

            def small_heads():
                def project_small(b):
                    for n in range(ST):
                        m = b * ST + n
                        for k in range(KT):
                            mm = pe.matmul(ps[:, 2 + n, 0:BCOLS], xnT[:, k, m * P:(m + 1) * P], wb[:, k],
                                           start=(k == 0), stop=(k == KT - 1))
                        mm.then_inc(b_mm, 1)

                turn_xn(2, 0)
                pe.wait_ge(xnT_ready, 2 * NT // 2 + ST // 2)
                pe.wait_ge(ld_bw, 2 * 16)
                project_small(0)
                turn_xn(2, 1)
                pe.wait_ge(xnT_ready, 3 * NT // 2)

                def step(s, r, i=None):
                    if r < BH:
                        banks = bank_set(r)
                        for bank, tiles in enumerate(IN_BANK):
                            if r >= 2:
                                pe.wait_ge(b_pT, (s - 2) * 3 + bank + 1)
                            for i4 in tiles:
                                at = SCORE_AT[i4]
                                if i is None:
                                    q, k = bqT[:, r, i4 * P:(i4 + 1) * P], bkT[:, r // 4, 0:(i4 + 1) * P]
                                else:
                                    q = bqT[:, ds(i * 4 + r, 1), i4 * P:(i4 + 1) * P].rearrange("p a b -> p (a b)")
                                    k = bkT[:, ds(i + r // 4, 1), 0:(i4 + 1) * P].rearrange("p a b -> p (a b)")
                                pe.matmul(banks[:, at:at + (i4 + 1) * P], q, k, start=True, stop=False)
                                mm = pe.matmul(banks[:, at + i4 * P:at + (i4 + 1) * P], identb[:], maskb[:], start=False, stop=True)
                            mm.then_inc(b_s, 1)
                    if r >= 5 and (r - 2) % 4 == 3:
                        g = key_head(r - 5, i)
                        pe.wait_ge(b_pT, (s - 1) * 3)
                        pe.wait_ge(b_vc, g + (b * BKV + 1))
                        if r > 5 or b > 0:
                            pe.wait_ge(b_oT, g + b * BKV)
                        for j in range(ST):
                            for h in range(4):
                                at, w = TURNED_AT[j], S - j * P
                                mm = pe.matmul(ps[h * 32:(h + 1) * 32, 3, j * P:S], bvc[:, j], bpT[:, h, at:at + w],
                                               start=(j == 0), stop=(j == ST - 1))
                        mm.then_inc(b_pv, 1)
                    if 1 <= r <= BH:
                        pe.wait_ge(b_norm, s * ST)
                        banks = bank_set(r - 1)
                        for i4 in range(ST):
                            for j in range(i4 + 1):
                                src = SCORE_AT[i4] + j * P
                                at = TURNED_AT[j] + (i4 - j) * P
                                mm = pe.transpose(banks[:, at:at + P], bp[:, (r - 1) % 2, src:src + P], ident[:])
                        mm.then_inc(b_pturned, 1)

                def out_small(b):
                    for n in range(ST):
                        for g in range(BKV):
                            mm = pe.matmul(ps[:, SMALL_OUT[n], 0:D], boT[:, g, n * P:(n + 1) * P], wob[:, g],
                                           start=(g == 0), stop=(g == BKV - 1))
                        mm.then_inc(b_wo, 1)

                for b in range(B):
                    if b > 0:
                        pe.wait_ge(b_oT, b * BKV)
                        project_small(b)
                        pe.wait_ge(b_qkv, 2 * (b + 1))
                        out_small(b - 1)
                    for n in range(ST):
                        m = b * ST + n
                        banks = TURN_BANKS[n % 2]
                        pe.wait_ge(b_stack, 6 * (m // 2 + 1))
                        if b > 0 and n == 1:
                            pe.wait_ge(x_added, 2 * NT + ST * b)
                        if n >= 2:
                            pe.wait_ge(b_qkT, 3 * (m - 1))
                        for h in range(BH):
                            pe.transpose(ps[:, banks[h // 8], :].bitcast(BF16)[:, (h % 8) * P:(h % 8 + 1) * P],
                                         bqs[:, n % 2, h].rearrange("p a b -> p (a b)"), identb[:])
                        for h in range(BKV):
                            mm = pe.transpose(ps[:, banks[2], :].bitcast(BF16)[:, h * P:(h + 1) * P],
                                              bks[:, n % 2, h].rearrange("p a b -> p (a b)"), identb[:])
                        mm.then_inc(b_turned, 1)
                    pe.wait_ge(b_qkT, 3 * (b + 1) * ST)
                    small_steps(pe, b, step)
                pe.wait_ge(b_oT, B * BKV)
                out_small(B - 1)

            def experts(l):
                if l > 0:
                    for b in range(B):
                        turn_xn(3, b)
                pe.wait_ge(xnT_ready, (2 * l + 2) * NT // 2)
                if l == 0:
                    pe.wait_ge(ld_sh, 12 * 16)
                for n in range(NT):
                    for k in range(KT):
                        mm = pe.matmul(ps[:, 4, n * E:(n + 1) * E], xnT[:, k, n * P:(n + 1) * P], wr[:, k],
                                       start=(k == 0), stop=(k == KT - 1))
                mm.then_inc(r_mm, 1)
                def hidden_mm(c):
                    for bank, w in ((c % 2, wsg), (2 + c % 2, wsu)):
                        for k in range(KT):
                            mm = pe.matmul(ps[:, bank, :], w[:, k, (c % FT) * P:(c % FT + 1) * P],
                                           xnT[:, k, (c // FT) * S:(c // FT + 1) * S], start=(k == 0), stop=(k == KT - 1))
                        mm.then_inc(sh_mm, 1)

                tile = 0
                for c in range(EARLY):
                    if c == 3:
                        pe.wait_ge(chosen_done, l + 1)
                        pe.matmul(ps[:, 5, :], tri[:], chosen[:].rearrange("p n e -> p (n e)"), start=True, stop=False)
                        for d in range(1, NT):
                            mm = pe.matmul(ps[:, 5, d * E:], ones[:], chosen[:, 0:NT - d].rearrange("p n e -> p (n e)"),
                                           start=False, stop=(d == NT - 1))
                        mm.then_inc(pos_mm, 1)
                    if c >= 2:
                        pe.wait_ge(sh_up, l * EARLY + c - 1)
                    hidden_mm(c)
                    while tile < MARKED_BY[c]:
                        pe.wait_ge(marked, l * NT + tile + 1)
                        if tile == 0:
                            pe.matmul(ps[:, 4, 0:2 * GROUPS], identb[:], nought[:], start=True, stop=False)
                        for g in range(GROUPS):
                            mm = pe.matmul(ps[:, 4, 2 * g:2 * g + 2], mark[tile % 3][:, g * EG:(g + 1) * EG, :].rearrange("p e c -> p (e c)"),
                                           number[:, tile], start=False, stop=(tile == NT - 1 and g == GROUPS - 1))
                        mm.then_inc(mark_used, 1)
                        tile += 1
                if l == 0:
                    pe.wait_ge(ld_gu, 16)
                    pe.wait_ge(ld_dn, 16)
                pe.wait_ge(sh_up, (l + 1) * EARLY)
                pe.wait_ge(tokens_ready, l + 1)
                for it in range(GROUPS + 3):
                    if it < GROUPS:
                        g = it
                        pe.wait_ge(xg_in[g], (l + 1) * 16)
                        for k in range(KT):
                            mm = pe.transpose(ps[:, g % 2, k * P:(k + 1) * P], xg[:, g, k * P:(k + 1) * P], ident[:])
                        mm.then_inc(xg_turned, 1)
                    if 1 <= it <= GROUPS:
                        g, u = it - 1, l * GROUPS + it - 1
                        pe.wait_ge(xgT_done, u + 1)
                        if g >= 2:
                            pe.wait_ge(hg_done, 2 * u - 2)
                        for k in range(KT):
                            for e in range(EG):
                                mm = pe.matmul(ps[e * CAP:(e + 1) * CAP, 2 + g % 2, 0:2 * F], xgT[:, g % 2, k, e * CAP:(e + 1) * CAP],
                                               wgu[:, k, g * EG + e], start=(k == 0), stop=(k == KT - 1))
                        mm.then_inc(gu_mm, 1)
                    if 2 <= it <= GROUPS + 1:
                        g, u = it - 2, l * GROUPS + it - 2
                        pe.wait_ge(hg_done, 2 * u + 2)
                        if g >= 1:
                            pe.wait_ge(hgT_done, u)
                        pe.transpose(ps[:, 4, 0:P], hg[:, g % 2].rearrange("p c f -> p (c f)"), ident[:]).then_inc(hg_turned, 1)
                    if it >= 3:
                        g, u = it - 3, l * GROUPS + it - 3
                        pe.wait_ge(hgT_done, u + 1)
                        if g >= 2:
                            pe.wait_ge(yg_done, u - 1)
                        for e in range(EG):
                            mm = pe.matmul(ps[e * CAP:(e + 1) * CAP, 6 + g % 2, 0:D], hgT[:, g % 2, e * CAP:(e + 1) * CAP],
                                           wd[:, (g * EG + e) // 2], start=True, stop=True)
                        mm.then_inc(dn_mm, 1)
                pe.wait_ge(sh_h, (l + 1) * EARLY)
                pe.wait_ge(yg_done, (l + 1) * GROUPS)
                for n in range(NT):
                    if n == ST:
                        for c in range(EARLY, 8):
                            hidden_mm(c)
                        pe.wait_ge(sh_late, (l + 1) * (8 - EARLY))
                    if n >= 4:
                        pe.wait_ge(sd_add, l * NT + n - 3)
                    for f in range(FT):
                        mm = pe.matmul(ps[:, 4 + n % 4, 0:D], hsh[:, f, n * P:(n + 1) * P], wsd[:, f],
                                       start=(f == 0), stop=(f == FT - 1))
                    mm.then_inc(sd_mm, 1)

            experts(0)
            small_heads()
            experts(1)


def constants():
    f = np.float32
    inv = f(1) / (f(1e6) ** (np.arange(0, HD, 2, dtype=f) / f(HD)))
    ang = np.outer(np.arange(S, dtype=f), inv).astype(f)
    c, s = np.cos(ang).astype(f), np.sin(ang).astype(f)
    by_tile = lambda a: np.ascontiguousarray(a.reshape(ST, P, -1).transpose(1, 0, 2))
    bf = mybir.dt.np(BF16)
    mask = np.where(np.arange(P)[None, :] > np.arange(P)[:, None], f(-3e38), f(0))
    row = np.arange(P)
    inv = f(1) / (f(1e6) ** (np.arange(BD // 2, dtype=f) / f(BD // 2)))
    ang = np.outer(np.arange(S, dtype=f), inv).astype(f)
    bc, bs = np.cos(ang).astype(f), np.sin(ang).astype(f)
    for_both = lambda a: np.stack([by_tile(a * f(BD ** -0.5)), by_tile(a)], 2)
    return {
        "b_cos": for_both(np.concatenate([bc, bc], 1)),
        "b_sin": for_both(np.concatenate([-bs, bs], 1)),
        "iota": np.tile(np.arange(E, dtype=f), (P, 1)),
        "nought": np.zeros((P, 2 * GROUPS)).astype(bf),
        "near": np.tile(np.arange(CAP, dtype=f) - f(FAR), (P, 1)),
        "number": np.stack([np.tile(np.arange(NT), (P, 1)), np.tile(row[:, None], (1, NT))], 2).astype(f).astype(bf),
        "parity": np.stack([row // CAP % 2 == 0, row // CAP % 2 == 1], 1).astype(f),
        "tri": (row[:, None] < row[None, :]).astype(bf),
        "ones": np.ones((P, P)).astype(bf),
        "ident": np.eye(P, dtype=f),
        "identb": np.eye(P).astype(bf),
        "maskb": mask.astype(bf),
        "cosf": by_tile(np.concatenate([c, c], 1)),
        "sinf": by_tile(np.concatenate([-s, s], 1)),
    }


def laid_out(i):
    apart = np.concatenate([np.arange(0, HD, 2), np.arange(1, HD, 2)])
    w = np.asarray(i["L0_attn_a_w_qkv"])
    q = w[:H * HD].reshape(KV, REP, HD, D)[:, :, apart].reshape(KV, QC, D)
    gate = w[H * HD:2 * H * HD].reshape(KV, QC, D)
    k = w[2 * H * HD:2 * H * HD + KV * HD].reshape(KV, HD, D)[:, apart]
    v = w[2 * H * HD + KV * HD:].reshape(KV, HD, D)
    w = np.concatenate([q, k, v], 1)
    rows = lambda a: np.broadcast_to(np.asarray(a)[None], (P,) + np.asarray(a).shape)
    vec = np.stack([np.asarray(i[f"L0_attn_a_{n}"])[apart] for n in ("q_norm_w", "q_norm_b", "k_norm_w", "k_norm_b")])
    g = lambda n: np.asarray(i["L0_ffn_" + n])
    shared = lambda a: a.reshape(SF, KT, P).transpose(2, 1, 0)
    bw = [np.asarray(i["L0_attn_b_" + n]) for n in ("Wq", "Wk", "Wv", "bq", "bk", "bv", "Wo")]
    wo_b = bw[6].reshape(BKV, 4, BD, D)
    wo_b = np.concatenate([wo_b, np.zeros_like(wo_b)], 2).reshape(BKV, P, D)
    return {
        "w_bqkv": np.concatenate(bw[0:3], 1).reshape(KT, P, BCOLS).transpose(1, 0, 2),
        "b_bias": rows(np.concatenate(bw[3:6])),
        "w_bo": wo_b.transpose(1, 0, 2),
        "w_sgate": shared(g("sh_gate_w")),
        "w_sup": shared(g("sh_up_w")),
        "w_sdown": g("sh_down_w").transpose(0, 2, 1).reshape(FT, P, D).transpose(1, 0, 2),
        "w_router": g("router_w").reshape(E, KT, P).transpose(2, 1, 0),
        "rbias": rows(g("router_bias")),
        "w_gateup": np.concatenate([g("gate_w"), g("up_w")], 1).reshape(E, 2 * F, KT, P).transpose(3, 2, 0, 1),
        "w_down": g("down_w").transpose(0, 2, 1).reshape(E // 2, P, D).transpose(1, 0, 2),
        "x": np.asarray(i["L0_attn_a_x"]),
        "w_qkv": w.reshape(KV, COLS, KT, P).transpose(0, 3, 2, 1),
        "w_gate": gate.reshape(KV, QC, KT, P).transpose(0, 3, 2, 1),
        "w_o": np.asarray(i["L0_attn_a_w_o"]).T.reshape(H, P, D).transpose(1, 0, 2),
        "nvec": rows(vec),
    }


def kernel(**inputs):
    import concourse.bacc as bacc
    from concourse.bass_utils import run_bass_kernel_spmd

    nc = bacc.Bacc("TRN2", target_bir_lowering=False, num_devices=1)
    arrays = {n: np.ascontiguousarray(a) for n, a in {**laid_out(inputs), **constants()}.items()}
    t = {n: nc.dram_tensor(f"in_{n}", a.shape, mybir.dt.from_np(a.dtype), kind="ExternalInput").ap() for n, a in arrays.items()}
    out = nc.dram_tensor("out_x", (B, S, D), F32, kind="ExternalOutput").ap()
    program(nc, t, out)
    got = run_bass_kernel_spmd(nc, [{f"in_{n}": a for n, a in arrays.items()}], core_ids=[0])
    return got.results[0]["out_x"]
```
